# Optimizing a Trainium2 kernel written in Bass

```python
import numpy as np
import jax
import jax.numpy as jnp

def _softmax(x, axis=-1):
    return jax.nn.softmax(x, axis=axis)

def _gelu(x):
    return jax.nn.gelu(x, approximate=True)

def _silu(x):
    return jax.nn.silu(x)

def _sigmoid(x):
    return jax.nn.sigmoid(x)

def _layernorm(x, axis=-1, eps=1e-05):
    m = jnp.mean(x, axis=axis, keepdims=True)
    v = jnp.var(x, axis=axis, keepdims=True)
    return (x - m) / jnp.sqrt(v + eps)

def _scatter_add(tgt, idx, src, axis=0):
    return tgt.at[idx].add(src)

def _segment_sum(src, seg, n):
    return jax.ops.segment_sum(src, seg, n)
kernel_name = 'mk_gnn_preln_d2_gnn_r32_8db48f'

def setup_inputs(seed: int=0):
    np.random.seed(seed)
    _w = jnp.asarray

    def _rec_inputs():
        import jax
        import jax.numpy as jnp
        _gk = jax.random.key(seed)
        x = -6.415e-05 + 1 * jax.random.normal(jax.random.fold_in(_gk, 1), (625, 512), jnp.float32)
        src = jax.random.randint(jax.random.fold_in(_gk, 2), (10000,), 0, 625, jnp.int32)
        dst = jax.random.randint(jax.random.fold_in(_gk, 3), (10000,), 0, 625, jnp.int32)
        _o = jnp.argsort(dst, stable=True)
        src = src[_o]
        dst = dst[_o]
        edge_type_3 = jax.random.randint(jax.random.fold_in(_gk, 13), (10000,), 0, 3, jnp.int32)
        node_type_3 = jax.random.randint(jax.random.fold_in(_gk, 14), (625,), 0, 3, jnp.int32)
        return (x, src, dst, edge_type_3, node_type_3)
    x, src, dst, edge_type_3, node_type_3 = _rec_inputs()

    def _L0_gnn_setup():
        import jax, jax.numpy as jnp
        import numpy as np
        N_NODES = 625
        N_EDGES = 150000
        D_IN = 512
        D_OUT = 512
        N_REL = 3
        N_NT = 3
        key = jax.random.key(seed)
        ks = jax.random.split(key, 8)
        x = jax.random.normal(ks[0], (N_NODES, D_IN), dtype=jnp.float32)
        W_rel = jax.random.normal(ks[1], (N_REL, D_IN, D_OUT), dtype=jnp.float32) * 0.02
        b_rel = jnp.zeros((N_REL, D_OUT), dtype=jnp.float32)
        W_self = jax.random.normal(ks[2], (N_NT, D_IN, D_OUT), dtype=jnp.float32) * 0.02
        b_self = jnp.zeros((N_NT, D_OUT), dtype=jnp.float32)
        edge_src = jax.random.randint(ks[3], (N_EDGES,), 0, N_NODES, dtype=jnp.int32)
        edge_dst = jax.random.randint(ks[4], (N_EDGES,), 0, N_NODES, dtype=jnp.int32)
        edge_type = jax.random.randint(ks[5], (N_EDGES,), 0, N_REL, dtype=jnp.int32)
        node_type = jax.random.randint(ks[6], (N_NODES,), 0, N_NT, dtype=jnp.int32)
        return {'x': x, 'W_rel': W_rel, 'b_rel': b_rel, 'W_self': W_self, 'b_self': b_self, 'edge_src': edge_src, 'edge_dst': edge_dst, 'edge_type': edge_type, 'node_type': node_type}
    _L0_gnn_all = _L0_gnn_setup()
    _L0_gnn_in = {k: v for k, v in _L0_gnn_all.items() if k in ('W_rel', 'b_rel', 'W_self', 'b_self')}
    del _L0_gnn_all

    def _L1_gnn_setup():
        import jax, jax.numpy as jnp
        import numpy as np
        from math import sqrt
        N = 50000
        E = 25000
        D_EMB = 512
        DK = 64
        DV = 64
        HEADS = 8

        def _attention_message(Q, K, V, senders, receivers, n_nodes):
            scale = 1.0 / sqrt(Q.shape[-1])
            scores = jnp.einsum('ehd,ehd->eh', Q[receivers], K[senders]) * scale
            smax = jax.ops.segment_max(scores, receivers, num_segments=n_nodes)
            ex = jnp.exp(scores - smax[receivers])
            denom = jax.ops.segment_sum(ex, receivers, num_segments=n_nodes)
            att = ex / denom[receivers]
            out = jax.ops.segment_sum(att[:, :, None] * V[senders], receivers, num_segments=n_nodes)
            return (out, att)
        key = jax.random.key(seed)
        k1, k2, k3, k4 = jax.random.split(key, 4)
        x = jax.random.normal(k1, (N, D_EMB), dtype=jnp.float32)
        edge_index = jax.random.randint(k2, (2, E), 0, N, dtype=jnp.int64)
        out_qkv = (2 * DK + DV) * HEADS
        W_qkv = jax.random.normal(k3, (out_qkv, D_EMB), dtype=jnp.float32) / sqrt(D_EMB)
        b_qkv = jnp.zeros((out_qkv,), dtype=jnp.float32)
        W_ff = jax.random.normal(k4, (D_EMB, DV * HEADS), dtype=jnp.float32) / sqrt(DV * HEADS)
        b_ff = jnp.zeros((D_EMB,), dtype=jnp.float32)
        return {'x': x, 'edge_index': edge_index, 'W_qkv': W_qkv, 'b_qkv': b_qkv, 'W_ff': W_ff, 'b_ff': b_ff}
    _L1_gnn_all = _L1_gnn_setup()
    _L1_gnn_in = {k: v for k, v in _L1_gnn_all.items() if k in ('W_qkv', 'b_qkv', 'W_ff', 'b_ff')}
    del _L1_gnn_all
    return {'x': x, 'src': src, 'dst': dst, 'edge_type_3': edge_type_3, 'node_type_3': node_type_3, 'L0_gnn_W_rel': _L0_gnn_in['W_rel'], 'L0_gnn_b_rel': _L0_gnn_in['b_rel'], 'L0_gnn_W_self': _L0_gnn_in['W_self'], 'L0_gnn_b_self': _L0_gnn_in['b_self'], 'L1_gnn_W_qkv': _L1_gnn_in['W_qkv'], 'L1_gnn_b_qkv': _L1_gnn_in['b_qkv'], 'L1_gnn_W_ff': _L1_gnn_in['W_ff'], 'L1_gnn_b_ff': _L1_gnn_in['b_ff']}

def reference(x, src, dst, edge_type_3, node_type_3, L0_gnn_W_rel, L0_gnn_b_rel, L0_gnn_W_self, L0_gnn_b_self, L1_gnn_W_qkv, L1_gnn_b_qkv, L1_gnn_W_ff, L1_gnn_b_ff):
    import jax
    import jax.numpy as jnp

    def _L0_gnn_ref(x, W_rel, b_rel, W_self, b_self, edge_src, edge_dst, edge_type, node_type):
        import jax, jax.numpy as jnp
        import numpy as np
        N_NODES = 625
        N_EDGES = 150000
        D_IN = 512
        D_OUT = 512
        N_REL = 3
        N_NT = 3
        xr = jnp.einsum('nd,rde->rne', x, W_rel)
        msg = xr[edge_type, edge_src] + b_rel[edge_type]
        agg = jax.ops.segment_sum(msg, edge_dst, num_segments=N_NODES)
        xs = jnp.einsum('nd,tde->tne', x, W_self)
        h_self = xs[node_type, jnp.arange(N_NODES)] + b_self[node_type]
        return jax.nn.relu(h_self + agg)

    def _L1_gnn_ref(x, edge_index, W_qkv, b_qkv, W_ff, b_ff):
        import jax, jax.numpy as jnp
        import numpy as np
        from math import sqrt
        N = 50000
        E = 25000
        D_EMB = 512
        DK = 64
        DV = 64
        HEADS = 8

        def _attention_message(Q, K, V, senders, receivers, n_nodes):
            scale = 1.0 / sqrt(Q.shape[-1])
            scores = jnp.einsum('ehd,ehd->eh', Q[receivers], K[senders]) * scale
            smax = jax.ops.segment_max(scores, receivers, num_segments=n_nodes)
            ex = jnp.exp(scores - smax[receivers])
            denom = jax.ops.segment_sum(ex, receivers, num_segments=n_nodes)
            att = ex / denom[receivers]
            out = jax.ops.segment_sum(att[:, :, None] * V[senders], receivers, num_segments=n_nodes)
            return (out, att)
        n_nodes = x.shape[0]
        qkv = x @ W_qkv.T + b_qkv
        Q, K, V = jnp.split(qkv, [DK * HEADS, 2 * DK * HEADS], axis=-1)
        Q = Q.reshape(n_nodes, HEADS, DK)
        K = K.reshape(n_nodes, HEADS, DK)
        V = V.reshape(n_nodes, HEADS, DV)
        senders, receivers = (edge_index[0], edge_index[1])
        msg, _ = _attention_message(Q, K, V, senders, receivers, n_nodes)
        out = msg.reshape(n_nodes, HEADS * DV) @ W_ff.T + b_ff
        return out
    edge_index = jnp.stack([src, dst])
    h = jnp.maximum(_layernorm(x, axis=-1), 0.0)
    x = x + _L0_gnn_ref(h, L0_gnn_W_rel, L0_gnn_b_rel, L0_gnn_W_self, L0_gnn_b_self, src, dst, edge_type_3, node_type_3)
    h = jnp.maximum(_layernorm(x, axis=-1), 0.0)
    x = x + _L1_gnn_ref(h, edge_index, L1_gnn_W_qkv, L1_gnn_b_qkv, L1_gnn_W_ff, L1_gnn_b_ff)
    return x

_drawn_inputs = setup_inputs


def setup_inputs(seed=0):
    import zlib

    import numpy as np

    out = dict(_drawn_inputs(seed))
    spreads = {'L0_gnn_b_rel': (0.0, 0.1),
     'L0_gnn_b_self': (0.0, 0.1),
     'L1_gnn_b_qkv': (0.0, 0.1),
     'L1_gnn_b_ff': (0.0, 0.1)}
    factors = {}
    for name, (base, spread) in spreads.items():
        noise = np.random.default_rng([zlib.crc32(name.encode()), seed]).standard_normal(out[name].shape)
        drawn = base * np.exp(spread * noise) if base else spread * noise
        out[name] = jnp.asarray(drawn.astype(out[name].dtype))
    for name, factor in factors.items():
        out[name] = (out[name] * factor).astype(out[name].dtype)
    return out
```

```python
from contextlib import ExitStack

import concourse.bass as bass
from concourse import mybir

F32 = mybir.dt.float32
F32R = mybir.dt.float32r
F16 = mybir.dt.float16
F8 = mybir.dt.float8e4
I32 = mybir.dt.int32
ALU = mybir.AluOpType
ACT = mybir.ActivationFunctionType
AX = mybir.AxisListType

P = 128
BIG = 1.0e30
EPS = 1e-5
EXACT16 = 2048


def gnn_kernel(nc, x_d, src_d, dst_d, etype_d, ntype_d, wrel_d, brel_d, wself_d, bself_d,
               wqkv_d, bqkv_d, wff_d, bff_d, out_d):
    N, D = x_d.shape
    E = src_d.shape[0]
    R = wrel_d.shape[0]
    T = wself_d.shape[0]
    DK = 64
    H = D // DK
    KD = D // P
    NT = -(-N // P)
    NP = NT * P
    LAST = N - (NT - 1) * P
    EC = -(-E // P)
    ETAIL = E - (EC - 1) * P
    WIN = 32
    NW = NP // WIN
    G = 6
    HALF = NP // 2
    NWT = R + T
    SCALE = float(DK) ** -0.5
    assert (N, D, E, R, T) == (625, 512, 10000, 3, 3)

    with ExitStack() as ctx:
        def sb(name, shape, dt):
            return ctx.enter_context(nc.sbuf_tensor(name, shape, dt))

        def sem(name):
            return ctx.enter_context(nc.semaphore(name))

        xs = sb("xs", [P, NT, D], F32)
        ident = sb("ident", [P, P], F32)
        ident16 = sb("ident16", [P, P], F16)
        b0 = sb("b0", [R + T, D], F32)
        bv_rows = sb("bv_rows", [P, D], F32)
        bff_rows = sb("bff_rows", [P, D], F32)
        ybuf = sb("ybuf", [P, 2, D], F32)
        edges_i = sb("edges_i", [EC, 3, P], I32)
        edge_keys = sb("edge_keys", [P, 2, 96], F32)
        ntype_i = sb("ntype_i", [NT, P], I32)
        ntype_f = sb("ntype_f", [NT, P], F32)
        type_mask = sb("type_mask", [P, NT, T], F32)
        mask6 = sb("mask6", [P, NT, R + T], F16)
        sel6 = sb("sel6", [P, R, R + T], F16)
        cnt6 = sb("cnt6", [R + T, NP], F32)
        bqkv_r = sb("bqkv_r", [3 * KD, P], F32)
        bqk = sb("bqk", [P, 2 * KD], F32)
        chunk_mm = sb("chunk_mm", [EC, 2], F32)
        win_iota = sb("win_iota", [NW, 2], F32)
        c_iota = sb("c_iota", [NW, 2, EC], F32)
        cover = sb("cover", [NW, 3, EC], F32)
        win_c = sb("win_c", [NW, 4], F32)
        bounds = sb("bounds", [1, 3, 32], I32)
        bounds_f = sb("bounds_f", [1, 4, 32], F32)
        stats = sb("stats", [P, NT, 6], F32)
        mv = sb("mv", [P, 2, NT, 2], F32)
        rstd = sb("rstd", [P, 2, NT, 2], F32)
        eps_c = sb("eps_c", [P, 1], F32)
        mask_add = sb("mask_add", [P, NT, NP], F32)
        neg_max = sb("neg_max", [P, NT, H], F32)
        denom = sb("denom", [P, NT, H], F32)
        recip = sb("recip", [P, 2, H], F32)
        norm = sb("norm", [P, 2, H], F32)

        Z_BYTES = 2 * KD * NP * 4
        W_BYTES = 2 * KD * D * 4
        RAW_BYTES = KD * D * 4
        ctx.enter_context(nc.sbuf_tensor("arena", [P, 167936 // 4], F32))
        arena0 = nc.sbuf_base - 167936
        at_byte = {}

        def place(name, offset, shape, dt):
            t = nc.alloc_sbuf_tensor_at(name, shape, dt, offset=arena0 + offset)
            return t

        o_z1, o_z0 = 0, Z_BYTES
        o_w = 2 * Z_BYTES
        o_raw = o_w + 2 * W_BYTES
        o_r4 = o_raw + 2 * RAW_BYTES + 2048
        o_ss = o_r4 + 4 * 4 * D * 2 * 4
        hT = place("hT", o_z1, [P, 2, KD, NP], F32R)
        zT = [place("zT_even", o_z0, [P, 2, KD, NP], F32R), place("zT_odd", o_z1, [P, 2, KD, NP], F32R)]
        h2T = place("h2T", o_z1, [P, 2, KD, NP], F32R)
        w_hl = [place(f"w_hl{i}", o_w + i * W_BYTES, [P, 2, KD, D], F32R) for i in range(2)]
        raw = [place(f"raw{i}", o_raw + i * RAW_BYTES, [P, KD, D], F32) for i in range(2)]
        h16 = place("h16", o_r4, [P, 2, NT, D], F16)
        adjT = place("adjT", o_r4 + 10240, [P, NT, R, NP], F16)
        adjT_res = place("adjT_res", o_r4 + 29440, [P, NT, R, NP], F8)
        src_hot = place("src_hot", o_r4 + 39040, [P, G, NP], F16)
        dst_hot = place("dst_hot", o_r4 + 46720, [P, G, R, WIN], F16)
        iota = place("iota", o_r4 + 47872, [P, R, NP], F16)
        mcount = place("mcount", o_r4 + 51712, [P, 2, 512], F32)
        edges_f = place("edges_f", o_r4 + 51712, [EC, 2, P], F32)
        mlog = place("mlog", o_r4 + 55808, [P, 2, 512], F32)
        self_sum = place("self_sum", o_ss, [P, NT, D], F32)
        wqkvT = place("wqkvT", o_r4, [P, 2, KD, 3 * D], F32R)
        wffT = place("wffT", o_r4 + 49152, [P, 2, KD, D], F32R)
        q_st = place("q_st", o_z0, [P, H, NP], F32R)
        k_hi = place("k_hi", o_z0 + 20480, [P, H, NP], F32R)
        k_lo = place("k_lo", o_z0 + 40960, [P, H, NP], F32R)
        v_sb = place("v_sb", o_z0 + 61440, [P, NT, D], F32)
        qk_f = place("qk_f", o_ss, [P, 2, NP], F32)
        s_sb = place("s_sb", o_r4, [P, 2, NP], F32)
        p_sb = place("p_sb", o_r4 + 5120, [P, 4, NP], F32)
        pT = place("pT", o_r4 + 15360, [P, NT * H, P], F32)
        msg_f = place("msg_f", o_r4 + 35840, [P, KD, P], F32)
        r_sb = place("r_sb", o_r4 + 37888, [P, KD, P], F32)
        msgT = place("msgT", o_r4 + 39936, [P, 2, 2, KD, P], F32R)

        banks = ctx.enter_context(nc.psum_tensor("banks", [P, 8, 512], F32))

        s_fill = sem("s_fill")
        s_edges = sem("s_edges")
        s_nodes = sem("s_nodes")
        s_x = sem("s_x")
        s_bias = sem("s_bias")
        s_raw = [sem("s_raw0"), sem("s_raw1")]
        s_keys = sem("s_keys")
        s_prep = sem("s_prep")
        s_chain = sem("s_chain")
        s_hot = sem("s_hot")
        s_slot = sem("s_slot")
        s_win = sem("s_win")
        s_adj = sem("s_adj")
        s_res = sem("s_res")
        s_var = sem("s_var")
        s_std = sem("s_std")
        s_y = sem("s_y")
        s_h16hi = sem("s_h16hi")
        s_whi = sem("s_whi")
        s_wlo = sem("s_wlo")
        s_unit = sem("s_unit")
        s_uhi = sem("s_uhi")
        s_ufree = sem("s_ufree")
        s_gemm = sem("s_gemm")
        s_acc = sem("s_acc")
        s_mc = sem("s_mc")
        s_ln = sem("s_ln")
        s_h16lo = sem("s_h16lo")
        s_mask = sem("s_mask")
        s_qk = sem("s_qk")
        s_kcp = sem("s_kcp")
        s_kcl = sem("s_kcl")
        s_sc = sem("s_sc")
        s_smax = sem("s_smax")
        s_exp = sem("s_exp")
        s_tr = sem("s_tr")
        s_pta = sem("s_pta")
        s_ptd = sem("s_ptd")
        s_pv = sem("s_pv")
        s_norm = sem("s_norm")
        s_rb = sem("s_rb")
        s_rsb = sem("s_rsb")
        s_msg = sem("s_msg")
        s_mhi = sem("s_mhi")
        s_mlo = sem("s_mlo")
        s_ff = sem("s_ff")
        s_xb = sem("s_xb")
        s_x1 = sem("s_x1")
        s_fin = sem("s_fin")
        s_out = [sem("s_out0"), sem("s_out1")]

        units = []
        side = []
        for it in range(NT):
            units.append(("hT", it, 0))
        for t in range(T):
            for it in range(NT):
                units.append(("self", t, it))
        assert len(units) == NW
        n_side = len(units)
        units += [("cnt", half, 0) for half in range(2)]

        def z_units(r):
            return [("z", r, dt, half) for dt in range(KD) for half in range(2)]

        units += z_units(0) + z_units(1) + [("gemm", 0)] + z_units(2) + [("gemm", 1)]
        units += [("m", it, part) for it in range(NT) for part in range(2)]
        units += [("wt", g, kt) for g in range(3) for kt in range(KD)]
        units += [("gemm", 2), ("ln", 0), ("ln", 1), ("wt", 3, 0), ("wt", 3, 1), ("h2T", 0, 0), ("ln", 2),
                  ("wt", 3, 2), ("wt", 3, 3), ("h2T", 1, 0), ("ln", 3), ("v", 0, 0), ("h2T", 2, 0), ("ln", 4),
                  ("v", 1, 0), ("h2T", 3, 0), ("v", 2, 0), ("h2T", 4, 0), ("v", 3, 0), ("v", 4, 0)]
        units += [("q", a, half) for a in range(KD) for half in range(2)]
        units += [("k", a, half) for a in range(KD) for half in range(2)]
        schedule = units
        ring = [u for u in units if u[0] not in ("gemm", "ln")]
        number = {u: n for n, u in enumerate(ring)}

        def bank(u):
            return banks[:, 5 + number[u] % 3, :]

        act_units = [u for u in ring if u[0] in ("hT", "z", "wt", "h2T", "q", "k")]
        act_done = {u: n + 1 for n, u in enumerate(act_units)}
        m_units = [u for u in ring if u[0] == "m"]

        def m_cols(part):
            return (0, 4 * P) if part == 0 else (4 * P, P)

        attention = []
        for m in range(NT * H + 8):
            if m < NT * H:
                attention += [("score", m), ("smax", m), ("exp", m)]
            if 0 <= m - 2 < NT * H:
                attention.append(("turn", m - 2))
                attention += [("fill", f) for f in range(NT * NT * H // 4)
                              if (4 * f + 3) // NT == m - 2]
            if m >= 10 and (m - 10) % H == 0 and (m - 10) // H < NT:
                attention.append(("norm", (m - 10) // H))
                attention.append(("rb", (m - 10) // H))
            if m >= 5 and (m - 5) % 2 == 0 and (m - 5) // 2 < NT * KD:
                attention.append(("pv", (m - 5) // 2))
            if m >= 12 and (m - 12) % H == 0 and (m - 12) // H < NT:
                attention.append(("msg", (m - 12) // H))
            if m >= 13 and (m - 13) % H == 0 and (m - 13) // H < NT:
                attention.append(("ff", (m - 13) // H))
                attention.append(("out", (m - 13) // H))

        block = ctx.enter_context(nc.Block())

        @block.sync
        def _(sp):
            sp.wait_ge(s_fill, 3)
            for k, arr in enumerate((dst_d, etype_d, src_d)):
                k = (1, 2, 0)[k]
                sp.dma_start(edges_i[0:EC - 1, k, :],
                             arr[0:(EC - 1) * P].rearrange("(c p) -> c p", p=P)).then_inc(s_edges, 16)
                sp.dma_start(edges_i[EC - 1:EC, k, 0:ETAIL],
                             arr[(EC - 1) * P:E].rearrange("(c p) -> c p", c=1)).then_inc(s_edges, 16)
            for q in range(NWT + 4):
                if q >= 2 and q - 2 < NWT:
                    sp.wait_ge(s_wlo, q - 1)
                elif q >= 2:
                    sp.wait_ge(s_unit, number[("wt", q - 2 - NWT, KD - 1)] + 1)
                if q < T:
                    w = wself_d[q].rearrange("(k p) n -> p k n", p=P)
                elif q < NWT:
                    w = wrel_d[q - T].rearrange("(k p) n -> p k n", p=P)
                elif q < NWT + 3:
                    w = wqkv_d[(q - NWT) * D:(q - NWT + 1) * D, :].rearrange("(k p) n -> p k n", p=P)
                else:
                    w = wff_d.rearrange("(k p) n -> p k n", p=P)
                sp.dma_start(raw[q % 2][:], w).then_inc(s_raw[q % 2], 16)
            for it in range(NT):
                rows = P if it < NT - 1 else LAST
                sp.wait_ge(s_fin, it + 1)
                sp.dma_start(out_d[it * P:it * P + rows, :], ybuf[0:rows, it % 2, :]).then_inc(s_out[it % 2], 16)
            sp.wait_ge(s_out[0], 16 * -(-NT // 2))
            sp.wait_ge(s_out[1], 16 * (NT // 2))

        @block.gpsimd
        def _(pool):
            nc.gpsimd.memset(edges_i[:, 0, :], 0).then_inc(s_fill, 1)
            nc.gpsimd.memset(edges_i[:, 1, :], N - 1).then_inc(s_fill, 1)
            nc.gpsimd.memset(edges_i[:, 2, :], R).then_inc(s_fill, 1)
            nc.gpsimd.memset(ntype_i[:], 0).then_inc(s_fill, 1)
            nc.gpsimd.memset(xs[:, NT - 1, :], 0.0).then_inc(s_fill, 1)
            nc.gpsimd.memset(ident[:], 0.0).then_inc(s_fill, 1)
            pool.wait_ge(s_fill, 6)
            nc.gpsimd.affine_select(out=ident[:], in_=ident[:], compare_op=ALU.not_equal, fill=1.0, base=0,
                                    pattern=[[-1, P]], channel_multiplier=1).then_inc(s_fill, 1)
            nc.gpsimd.iota(win_iota[:], [[WIN, 2]], base=0, channel_multiplier=WIN,
                           allow_small_or_imprecise_dtypes=True).then_inc(s_fill, 1)
            nc.gpsimd.iota(c_iota[:, 0, :], [[1, EC]], base=1, channel_multiplier=0,
                           allow_small_or_imprecise_dtypes=True).then_inc(s_fill, 1)
            nc.gpsimd.iota(c_iota[:, 1, :], [[-1, EC]], base=EC, channel_multiplier=0,
                           allow_small_or_imprecise_dtypes=True).then_inc(s_fill, 1)
            nc.gpsimd.memset(edge_keys[:], -1.0).then_inc(s_fill, 1)
            nc.gpsimd.iota(iota[:], [[1, R * NP]], base=0, channel_multiplier=0,
                           allow_small_or_imprecise_dtypes=True).then_inc(s_fill, 1)
            pool.wait_ge(s_fill, 7)
            nc.gpsimd.tensor_copy(ident16[:], ident[:]).then_inc(s_fill, 1)
            nc.gpsimd.memset(sel6[:], 0.0).then_inc(s_fill, 1)
            nc.gpsimd.memset(mask6[:], 0.0).then_inc(s_fill, 1)
            nc.gpsimd.memset(eps_c[:], EPS).then_inc(s_fill, 1)
            pool.wait_ge(s_fill, 14)
            for r in range(R):
                nc.gpsimd.memset(sel6[:, r, r:r + 1], 1.0).then_inc(s_fill, 1)
            for q in range(NWT):
                pool.wait_ge(s_whi, q + 1)
                nc.gpsimd.tensor_tensor(w_hl[q % 2][:, 1], raw[q % 2][:], w_hl[q % 2][:, 0].bitcast(F32),
                                        ALU.subtract).then_inc(s_wlo, 1)
            for n, u in enumerate(m_units):
                _, it, part = u
                c0, cn = m_cols(part)
                pool.wait_ge(s_ln, n + 1)
                pool.wait_ge(s_ufree, number[u] + 1)
                nc.gpsimd.tensor_tensor(mask_add[:, it, c0:c0 + cn], mask_add[:, it, c0:c0 + cn],
                                        mlog[:, n % 2, 0:cn], ALU.subtract).then_inc(s_mask, 1)
            for it in range(NT):
                pool.wait_ge(s_bias, 80)
                pool.wait_ge(s_y, NT + it + 1)
                nc.gpsimd.tensor_tensor(xs[:, it, :], xs[:, it, :], bff_rows[:], ALU.add).then_inc(s_xb, 1)
            pool.wait_ge(s_xb, NT)
            for a in range(KD):
                pool.wait_ge(s_qk, 4 * KD + 4 * (a + 1))
                for hh in range(2):
                    me, other = 64 * hh, 64 - 64 * hh
                    if a or hh:
                        pool.wait_ge(s_kcl, 2 * a + hh)
                    nc.gpsimd.tensor_copy(k_lo[other:other + 64, 2 * a + hh, :],
                                          k_lo[me:me + 64, 2 * a + hh, :].bitcast(F32)).then_inc(s_kcl, 1)
            for it in range(NT):
                if it == 0:
                    pool.wait_ge(s_kcl, 2 * KD)
                pool.wait_ge(s_mhi, it + 1)
                nc.gpsimd.tensor_tensor(msgT[:, it % 2, 1], msg_f[:], msgT[:, it % 2, 0].bitcast(F32),
                                        ALU.subtract).then_inc(s_mlo, 1)

        @block.scalar
        def _(act):
            act.wait_ge(s_fill, 5)
            act.dma_start(xs[:, 0:NT - 1, :], x_d[0:(NT - 1) * P, :].rearrange("(t p) d -> p t d", p=P)
                          ).then_inc(s_x, 16)
            act.dma_start(xs[0:LAST, NT - 1, :], x_d[(NT - 1) * P:N, :]).then_inc(s_x, 16)
            act.dma_start(ntype_i[0:NT - 1, :], ntype_d[0:(NT - 1) * P].rearrange("(t p) -> t p", p=P)
                          ).then_inc(s_nodes, 16)
            act.dma_start(ntype_i[NT - 1:NT, 0:LAST], ntype_d[(NT - 1) * P:N].rearrange("(t p) -> t p", t=1)
                          ).then_inc(s_nodes, 16)
            act.dma_start(b0[0:R, :], brel_d).then_inc(s_bias, 16)
            act.dma_start(b0[R:R + T, :], bself_d).then_inc(s_bias, 16)
            act.dma_start(bqkv_r[:], bqkv_d.rearrange("(o p) -> o p", p=P)).then_inc(s_bias, 16)
            act.dma_start(bv_rows[:], bqkv_d[2 * D:3 * D].partition_broadcast(P)).then_inc(s_bias, 16)
            act.dma_start(bff_rows[:], bff_d.partition_broadcast(P)).then_inc(s_bias, 16)

            def weights_hi(q):
                act.wait_ge(s_raw[q % 2], 16 * (q // 2 + 1))
                if q - 2 >= T:
                    act.wait_ge(s_gemm, q - 2 - T + 1)
                elif q >= 2:
                    act.wait_ge(s_unit, number[("self", q - 2, NT - 1)] + 1)
                nc.scalar.activation(w_hl[q % 2][:, 0], raw[q % 2][:], ACT.Copy).then_inc(s_whi, 1)

            def standard_deviation(layer, t0, t1, count):
                act.wait_ge(s_var, count)
                nc.scalar.activation(rstd[:, layer, t0:t1, 0], mv[:, layer, t0:t1, 1], ACT.Sqrt,
                                     bias=eps_c[:]).then_inc(s_std, 1)

            def store_window(w):
                act.wait_ge(s_win, w + 1)
                nc.scalar.activation(adjT[:, :, :, w * WIN:(w + 1) * WIN],
                                     banks[:, w % 2, 0:NT * R * WIN].rearrange("p (t r i) -> p t r i", t=NT, r=R),
                                     ACT.Copy).then_inc(s_adj, 1)

            weights_hi(0)
            act.wait_ge(s_fill, 19)
            standard_deviation(0, 0, NT, 1)
            for it in range(NT):
                act.wait_ge(s_y, it + 1)
                nc.scalar.activation(h16[:, 0, it, :], self_sum[:, it, :], ACT.Relu).then_inc(s_h16hi, 1)

            def unit_part(u):
                kind = u[0]
                if kind not in ("hT", "z", "wt", "h2T", "q", "k"):
                    return
                act.wait_ge(s_unit, number[u] + 1)
                if kind == "hT":
                    it = u[1]
                    ins = nc.scalar.activation(hT[:, 0, :, it * P:(it + 1) * P],
                                               bank(u).rearrange("p (k i) -> p k i", k=KD), ACT.Relu)
                elif kind == "h2T":
                    it = u[1]
                    ins = nc.scalar.activation(h2T[:, 0, :, it * P:(it + 1) * P],
                                               bank(u).rearrange("p (k i) -> p k i", k=KD), ACT.Relu)
                elif kind == "z":
                    _, r, dt, half = u
                    ins = nc.scalar.activation(zT[r % 2][:, 0, dt, half * HALF:(half + 1) * HALF],
                                               bank(u)[:, 0:HALF], ACT.Copy)
                elif kind == "wt":
                    _, g, kt = u
                    if u == ("wt", 0, 0):
                        act.wait_ge(s_mask, len(m_units))
                    to = wqkvT[:, 0, kt, g * D:(g + 1) * D] if g < 3 else wffT[:, 0, kt, :]
                    ins = nc.scalar.activation(to, bank(u), ACT.Copy)
                else:
                    _, a, half = u
                    n = a if kind == "q" else KD + a
                    if n == 0:
                        act.wait_ge(s_keys, 14)
                    if n >= 2:
                        act.wait_ge(s_qk, 4 * (n - 1))
                    ins = nc.scalar.activation(qk_f[:, n % 2, half * HALF:(half + 1) * HALF], bank(u)[:, 0:HALF],
                                               ACT.Identity, bias=bqk[:, n:n + 1],
                                               scale=-SCALE if kind == "q" else 1.0)
                ins.then_inc(s_uhi, 1)

            w_at = {2: 1, 11: 2, 15: 3}
            for w in range(NW):
                store_window(w)
                if w in w_at:
                    weights_hi(w_at[w])
                if w >= 1:
                    unit_part(ring[w - 1])
            unit_part(ring[NW - 1])
            pending = {("z", 1, 0, 0): 4, ("z", 2, 0, 0): 5}
            n_ln = 0
            for u in schedule[n_side:]:
                if u in pending:
                    weights_hi(pending[u])
                if u[0] == "m":
                    cn = m_cols(u[2])[1]
                    act.wait_ge(s_mc, n_ln + 1)
                    if n_ln >= 2:
                        act.wait_ge(s_mask, n_ln - 1)
                    nc.scalar.activation(mlog[:, n_ln % 2, 0:cn], mcount[:, n_ln % 2, 0:cn], ACT.Ln
                                         ).then_inc(s_ln, 1)
                    n_ln += 1
                    continue
                if u[0] == "ln":
                    standard_deviation(1, u[1], u[1] + 1, 2 + u[1])
                    continue
                if u[0] == "gemm":
                    continue
                unit_part(u)
                if u[0] == "k" and u[2] == 1:
                    a = u[1]
                    for hh in range(2):
                        me, other = 64 * hh, 64 - 64 * hh
                        act.wait_ge(s_qk, 4 * KD + 4 * a + hh + 1)
                        nc.scalar.activation(k_hi[other:other + 64, 2 * a + hh, :],
                                             k_hi[me:me + 64, 2 * a + hh, :].bitcast(F32), ACT.Copy
                                             ).then_inc(s_kcp, 1)

            for step in attention:
                kind, n = step
                if kind == "exp":
                    it, h = divmod(n, H)
                    act.wait_ge(s_smax, n + 1)
                    if n >= 4:
                        act.wait_ge(s_tr, -(-(n - 3) * NT // 4))
                    nc.scalar.activation(p_sb[:, n % 4, :], s_sb[:, n % 2, :], ACT.Exp, scale=-1.0,
                                         bias=neg_max[:, it, h:h + 1],
                                         accum_out=denom[:, it, h:h + 1]).then_inc(s_exp, 1)
                elif kind == "fill" and n % 2 == 0:
                    act.wait_ge(s_tr, n + 1)
                    if 4 * n + 3 >= NT * H:
                        act.wait_ge(s_pv, (4 * n + 3 - NT * H) // (2 * NT) + 1)
                    nc.scalar.activation(pT[:, 4 * n % (NT * H):4 * n % (NT * H) + 4, :],
                                         banks[:, 5 + n % 2, :].rearrange("p (s i) -> p s i", s=4), ACT.Copy
                                         ).then_inc(s_pta, 1)
                elif kind == "rb":
                    act.wait_ge(s_rb, n + 1)
                    if n >= 1:
                        act.wait_ge(s_msg, n)
                    nc.scalar.activation(r_sb[:], banks[:, 7, :].rearrange("p (a i) -> p a i", a=KD), ACT.Copy
                                         ).then_inc(s_rsb, 1)
                elif kind == "msg":
                    act.wait_ge(s_msg, n + 1)
                    if n >= 2:
                        act.wait_ge(s_ff, n - 1)
                    nc.scalar.activation(msgT[:, n % 2, 0], msg_f[:], ACT.Copy).then_inc(s_mhi, 1)

        @block.vector
        def _(dve):
            links = [0]

            def chain(ins):
                links[0] += 1
                ins.then_inc(s_chain, 1)
                dve.wait_ge(s_chain, links[0])

            dve.wait_ge(s_edges, 96)
            dve.wait_ge(s_fill, 11)
            nc.vector.tensor_reduce(chunk_mm[:, 0:1], edges_i[:, 1, :], AX.X, ALU.min).then_inc(s_keys, 1)
            nc.vector.tensor_reduce(chunk_mm[:, 1:2], edges_i[:, 1, :], AX.X, ALU.max).then_inc(s_keys, 1)
            nc.vector.tensor_copy(edges_f[:, 0, :], edges_i[:, 0, :]).then_inc(s_keys, 1)
            nc.vector.scalar_tensor_tensor(out=edges_f[:, 1, :], in0=edges_i[:, 2, :], scalar=float(NP),
                                           in1=edges_i[:, 1, :], op0=ALU.mult, op1=ALU.add).then_inc(s_keys, 1)
            dve.wait_ge(s_nodes, 32)
            nc.vector.tensor_copy(ntype_f[:], ntype_i[:]).then_inc(s_keys, 1)
            dve.wait_ge(s_prep, 1)
            low = banks[0:NW, 2, 0:EC]
            high = banks[0:NW, 2, EC:2 * EC]
            chain(nc.vector.tensor_scalar(cover[:, 0, :], low, win_iota[:, 1:2], None, ALU.is_lt))
            chain(nc.vector.scalar_tensor_tensor(out=cover[:, 1, :], in0=high, scalar=win_iota[:, 0:1],
                                                 in1=cover[:, 0, :], op0=ALU.is_ge, op1=ALU.mult))
            chain(nc.vector.tensor_tensor_reduce(cover[:, 2, :], cover[:, 1, :], c_iota[:, 0, :], 1.0, 0.0,
                                                 ALU.mult, ALU.max, win_c[:, 1:2]))
            chain(nc.vector.tensor_tensor_reduce(cover[:, 2, :], cover[:, 1, :], c_iota[:, 1, :], 1.0, 0.0,
                                                 ALU.mult, ALU.max, win_c[:, 0:1]))
            chain(nc.vector.tensor_scalar(win_c[:, 0:1], win_c[:, 0:1], -1.0, float(EC), ALU.mult, ALU.add))
            nc.vector.tensor_scalar(win_c[:, 2:3], win_c[:, 0:1], float(EC - 1), None, ALU.min).then_inc(s_keys, 1)
            dve.wait_ge(s_prep, 2)
            brow = banks[0:1, 3, 0:2 * NW]
            chain(nc.vector.tensor_copy(bounds_f[:, 0:2, 0:NW], brow.rearrange("p (b w) -> p b w", b=2)))
            chain(nc.vector.scalar_tensor_tensor(out=bounds_f[:, 2, 0:NW], in0=bounds_f[:, 0, 0:NW], scalar=1.0,
                                                 in1=bounds_f[:, 1, 0:NW], op0=ALU.add, op1=ALU.max))
            chain(nc.vector.tensor_tensor(bounds_f[:, 3, 0:NW], bounds_f[:, 2, 0:NW], bounds_f[:, 0, 0:NW],
                                          ALU.subtract))
            chain(nc.vector.tensor_reduce(bounds_f[:, 3, 31:32], bounds_f[:, 3, 0:NW], AX.X, ALU.max))
            nc.vector.tensor_copy(bounds[:, 0, 0:NW], bounds_f[:, 0, 0:NW]).then_inc(s_keys, 1)
            nc.vector.tensor_copy(bounds[:, 1, 0:NW], bounds_f[:, 2, 0:NW]).then_inc(s_keys, 1)
            nc.vector.tensor_copy(bounds[:, 2, 0:1], bounds_f[:, 3, 31:32]).then_inc(s_keys, 1)
            dve.wait_ge(s_prep, 3)
            chain(nc.vector.tensor_copy(edge_keys[:, :, 0:EC],
                                        banks[:, 4, 0:2 * EC].rearrange("p (k c) -> p k c", k=2)))
            for t in range(T):
                nc.vector.tensor_scalar(type_mask[:, :, t], banks[:, 4, 160:160 + NT], float(t), None,
                                        ALU.is_equal).then_inc(s_keys, 1)
            nc.vector.tensor_scalar(bqk[:, 0:KD], banks[:, 4, 176:176 + KD], -SCALE, None, ALU.mult
                                    ).then_inc(s_keys, 1)
            nc.vector.tensor_copy(bqk[:, KD:2 * KD], banks[:, 4, 176 + KD:176 + 2 * KD]).then_inc(s_keys, 1)
            dve.wait_ge(s_fill, 19)
            dve.wait_ge(s_keys, 12)
            nc.vector.tensor_copy(mask6[:, :, R:R + T], type_mask[:]).then_inc(s_keys, 1)

            def statistics(layer, it):
                chain(nc.vector.bn_stats(stats[:, it, :], xs[:, it, :]))
                return nc.vector.bn_aggr(mv[:, layer, it, :], stats[:, it, :])

            def normalise(layer, it, to):
                nc.vector.tensor_scalar(to, xs[:, it, :], mv[:, layer, it, 0:1], rstd[:, layer, it, 1:2],
                                        ALU.subtract, ALU.mult).then_inc(s_y, 1)

            dve.wait_ge(s_x, 32)
            for it in range(NT):
                ins = statistics(0, it)
            ins.then_inc(s_var, 1)
            dve.wait_ge(s_std, 1)
            chain(nc.vector.reciprocal(rstd[:, 0, :, 1], rstd[:, 0, :, 0]))
            for it in range(NT):
                normalise(0, it, self_sum[:, it, :])

            lo = load_bounds(dve, nc, bounds, 0, NW, EC)
            hi = load_bounds(dve, nc, bounds, 1, NW, EC)
            widest = dve.value_load(bounds[0:1, 2, 0:1], min_val=1, max_val=EC)
            asked = dve.alloc_register()
            dve.reg_mov(asked, G // 2)

            def one_hots(w):
                with dve.Fori(lo[w], hi[w], G) as c:
                    for k in range(G):
                        if k % (G // 2) == 0:
                            dve.wait_ge(s_slot, dve.snap(asked, min_val=1, max_val=1 << 20))
                            dve.reg_add(asked, asked, G // 2)
                        nc.vector.tensor_scalar(src_hot[:, k, :], iota[:, 0, :],
                                                edge_keys[:, 0, bass.ds(c + k, 1)], None, ALU.is_equal
                                                ).then_inc(s_hot, 1)
                        nc.vector.tensor_scalar(dst_hot[:, k, :, :], iota[:, :, w * WIN:(w + 1) * WIN],
                                                edge_keys[:, 1, bass.ds(c + k, 1)], None, ALU.is_equal
                                                ).then_inc(s_hot, 1)

            def residual(w):
                dve.wait_ge(s_adj, w + 1)
                with dve.If(widest > EXACT16 // P):
                    nc.vector.tensor_tensor(
                        adjT_res[:, :, :, w * WIN:(w + 1) * WIN],
                        banks[:, w % 2, 0:NT * R * WIN].rearrange("p (t r i) -> p t r i", t=NT, r=R),
                        adjT[:, :, :, w * WIN:(w + 1) * WIN], ALU.subtract, saturate=False)
                nc.vector.engine_nop().then_inc(s_res, 1)

            def unit_part(u):
                kind = u[0]
                b = bank(u)
                dve.wait_ge(s_unit, number[u] + 1)
                if u in act_done:
                    dve.wait_ge(s_uhi, act_done[u])
                if kind in ("hT", "h2T"):
                    it = u[1]
                    to = hT if kind == "hT" else h2T
                    nc.vector.scalar_tensor_tensor(
                        out=to[:, 1, :, it * P:(it + 1) * P], in0=b.rearrange("p (k i) -> p k i", k=KD), scalar=0.0,
                        in1=to[:, 0, :, it * P:(it + 1) * P].bitcast(F32), op0=ALU.max, op1=ALU.subtract
                    ).then_inc(s_ufree, 1)
                elif kind == "self":
                    _, t, it = u
                    m = type_mask[:, it, t:t + 1]
                    if t == 0:
                        nc.vector.tensor_scalar(self_sum[:, it, :], b, m, None, ALU.mult).then_inc(s_ufree, 1)
                    else:
                        dve.wait_ge(s_ufree, number[("self", t - 1, it)] + 1)
                        nc.vector.scalar_tensor_tensor(out=self_sum[:, it, :], in0=b, scalar=m,
                                                       in1=self_sum[:, it, :], op0=ALU.mult, op1=ALU.add
                                                       ).then_inc(s_ufree, 1)
                elif kind == "cnt":
                    half = u[1]
                    nc.vector.tensor_copy(cnt6[:, half * HALF:(half + 1) * HALF], b[0:R + T, 0:HALF]
                                          ).then_inc(s_ufree, 1)
                elif kind == "z":
                    _, r, dt, half = u
                    cols = slice(half * HALF, (half + 1) * HALF)
                    nc.vector.tensor_tensor(zT[r % 2][:, 1, dt, cols], b[:, 0:HALF],
                                            zT[r % 2][:, 0, dt, cols].bitcast(F32), ALU.subtract
                                            ).then_inc(s_ufree, 1)
                elif kind == "wt":
                    _, g, kt = u
                    to = (lambda part: wqkvT[:, part, kt, g * D:(g + 1) * D]) if g < 3 else \
                         (lambda part: wffT[:, part, kt, :])
                    nc.vector.tensor_tensor(to(1), b, to(0).bitcast(F32), ALU.subtract).then_inc(s_ufree, 1)
                elif kind == "m":
                    _, it, part = u
                    n = m_units.index(u)
                    c0, cn = m_cols(part)
                    if n >= 2:
                        dve.wait_ge(s_ln, n - 1)
                    nc.vector.tensor_scalar(mcount[:, n % 2, 0:cn], b[:, 0:cn], 1.0, None, ALU.max
                                            ).then_inc(s_mc, 1)
                    nc.vector.tensor_scalar(mask_add[:, it, c0:c0 + cn], b[:, 0:cn], 0.0, BIG,
                                            ALU.is_equal, ALU.mult).then_inc(s_ufree, 1)
                elif kind == "v":
                    jt = u[1]
                    dve.wait_ge(s_bias, 80)
                    nc.vector.tensor_tensor(v_sb[:, jt, :], b, bv_rows[:], ALU.add).then_inc(s_ufree, 1)
                elif kind == "q":
                    nc.vector.engine_nop().then_inc(s_ufree, 1)
                    if u[2] == 1:
                        split_q(u[1])
                else:
                    nc.vector.engine_nop().then_inc(s_ufree, 1)
                    if u[2] == 1:
                        split_k(u[1])

            def h16_lo(it):
                dve.wait_ge(s_h16hi, it + 1)
                nc.vector.scalar_tensor_tensor(out=h16[:, 1, it, :], in0=self_sum[:, it, :], scalar=0.0,
                                               in1=h16[:, 0, it, :], op0=ALU.max, op1=ALU.subtract
                                               ).then_inc(s_h16lo, 1)

            def split_q(a):
                f = qk_f[:, a % 2, :]
                for hh in range(2):
                    me = 64 * hh
                    nc.vector.tensor_copy(q_st[me:me + 64, 2 * a + hh, :], f[me:me + 64]).then_inc(s_qk, 1)
                for hh in range(2):
                    me, other = 64 * hh, 64 - 64 * hh
                    dve.wait_ge(s_qk, 4 * a + hh + 1)
                    nc.vector.tensor_tensor(q_st[other:other + 64, 2 * a + hh, :], f[me:me + 64],
                                            q_st[me:me + 64, 2 * a + hh, :].bitcast(F32), ALU.subtract
                                            ).then_inc(s_qk, 1)

            def split_k(a):
                f = qk_f[:, (KD + a) % 2, :]
                for hh in range(2):
                    me = 64 * hh
                    nc.vector.tensor_copy(k_hi[me:me + 64, 2 * a + hh, :], f[me:me + 64]).then_inc(s_qk, 1)
                for hh in range(2):
                    me = 64 * hh
                    dve.wait_ge(s_qk, 4 * (KD + a) + hh + 1)
                    nc.vector.tensor_tensor(k_lo[me:me + 64, 2 * a + hh, :], f[me:me + 64],
                                            k_hi[me:me + 64, 2 * a + hh, :].bitcast(F32), ALU.subtract
                                            ).then_inc(s_qk, 1)

            for w in range(NW):
                one_hots(w)
                if w >= 1:
                    residual(w - 1)
                    unit_part(ring[w - 1])
                    if w - 1 < NT:
                        h16_lo(w - 1)
            residual(NW - 1)
            unit_part(ring[NW - 1])

            for u in schedule[n_side:]:
                if u[0] == "ln":
                    it = u[1]
                    dve.wait_ge(s_acc, it + 1)
                    chain(nc.vector.tensor_tensor(self_sum[:, it, :], banks[:, it, :], self_sum[:, it, :],
                                                  ALU.add))
                    chain(nc.vector.scalar_tensor_tensor(out=xs[:, it, :], in0=self_sum[:, it, :], scalar=0.0,
                                                         in1=xs[:, it, :], op0=ALU.max, op1=ALU.add))
                    statistics(1, it).then_inc(s_var, 1)
                    dve.wait_ge(s_std, 2 + it)
                    chain(nc.vector.reciprocal(rstd[:, 1, it, 1:2], rstd[:, 1, it, 0:1]))
                    if it >= 2:
                        dve.wait_ge(s_unit, number[("h2T", it - 2, 0)] + 1)
                    normalise(1, it, ybuf[:, it % 2, :])
                elif u[0] != "gemm":
                    unit_part(u)

            for step in attention:
                kind, n = step
                if kind == "smax":
                    it, h = divmod(n, H)
                    dve.wait_ge(s_sc, n + 1)
                    dve.wait_ge(s_mask, 2 * (it + 1))
                    if n >= 2:
                        dve.wait_ge(s_exp, n - 1)
                    c = 2 * (n % 2)
                    nc.vector.tensor_tensor_reduce(
                        s_sb[:, n % 2, :].rearrange("p (a j) -> p a j", a=2), banks[:, c:c + 2, 0:HALF],
                        mask_add[:, it, :].rearrange("p (a j) -> p a j", a=2), 1.0, 3.0e38, ALU.add, ALU.min,
                        neg_max[:, it, h:h + 1]).then_inc(s_smax, 1)
                elif kind == "fill" and n % 2 == 1:
                    dve.wait_ge(s_tr, n + 1)
                    if 4 * n + 3 >= NT * H:
                        dve.wait_ge(s_pv, (4 * n + 3 - NT * H) // (2 * NT) + 1)
                    nc.vector.tensor_copy(pT[:, 4 * n % (NT * H):4 * n % (NT * H) + 4, :],
                                          banks[:, 5 + n % 2, :].rearrange("p (s i) -> p s i", s=4)
                                          ).then_inc(s_ptd, 1)
                elif kind == "norm":
                    dve.wait_ge(s_exp, H * (n + 1))
                    if n >= 2:
                        dve.wait_ge(s_rb, n - 1)
                    chain(nc.vector.reciprocal(recip[:, n % 2, :], denom[:, n, :]))
                    nc.vector.scalar_tensor_tensor(out=norm[:, n % 2, :], in0=neg_max[:, n, :], scalar=BIG / 2,
                                                   in1=recip[:, n % 2, :], op0=ALU.is_lt, op1=ALU.mult
                                                   ).then_inc(s_norm, 1)
                elif kind == "msg":
                    dve.wait_ge(s_pv, KD * (n + 1))
                    dve.wait_ge(s_rsb, n + 1)
                    if n >= 1:
                        dve.wait_ge(s_mlo, n)
                    nc.vector.tensor_tensor(msg_f[:], banks[:, 4, :].rearrange("p (a i) -> p a i", a=KD), r_sb[:],
                                            ALU.mult).then_inc(s_msg, 1)
                elif kind == "out":
                    dve.wait_ge(s_ff, n + 1)
                    dve.wait_ge(s_xb, n + 1)
                    if n >= 2:
                        dve.wait_ge(s_out[n % 2], 16 * (n // 2))
                    nc.vector.tensor_tensor(ybuf[:, n % 2, :], banks[:, 7, :], xs[:, n, :], ALU.add
                                            ).then_inc(s_fin, 1)

        @block.tensor
        def _(pe):
            mm = nc.tensor.matmul
            PASSES = ((0, 0), (0, 1), (1, 0))

            pe.wait_ge(s_fill, 7)
            pe.wait_ge(s_keys, 2)
            for k in range(2):
                ins = mm(banks[0:NW, 2, k * EC:(k + 1) * EC], chunk_mm[:, k:k + 1].broadcast_to([EC, NW]),
                         ident[0:EC, 0:EC], start=(k == 0), stop=True, skip_group_check=True)
            ins.then_inc(s_prep, 1)
            pe.wait_ge(s_keys, 6)
            for k, col in enumerate((2, 1)):
                ins = mm(banks[0:1, 3, k * NW:(k + 1) * NW], win_c[:, col:col + 1], ident[0:NW, 0:NW],
                         start=(k == 0), stop=True, skip_group_check=True)
            ins.then_inc(s_prep, 1)
            for k in range(2):
                nc.tensor.transpose(banks[:, 4, k * EC:(k + 1) * EC], edges_f[:, k, :], ident[0:EC, 0:EC])
            nc.tensor.transpose(banks[:, 4, 160:160 + NT], ntype_f[:], ident[0:NT, 0:NT])
            pe.wait_ge(s_bias, 80)
            nc.tensor.transpose(banks[:, 4, 176:176 + 3 * KD], bqkv_r[:], ident[0:3 * KD, 0:3 * KD]
                                ).then_inc(s_prep, 1)

            pe.wait_ge(s_keys, 9)
            lo = load_bounds(pe, nc, bounds, 0, NW, EC)
            hi = load_bounds(pe, nc, bounds, 1, NW, EC)
            widest = pe.value_load(bounds[0:1, 2, 0:1], min_val=1, max_val=EC)
            pe.sem_inc(s_slot, G)
            filled = pe.alloc_register()
            pe.reg_mov(filled, G)

            def turn(w, first):
                for k in range(G):
                    if k % (G // 2) == 0:
                        pe.wait_ge(s_hot, pe.snap(filled, min_val=1, max_val=1 << 20))
                        pe.reg_add(filled, filled, G)
                    for jt in range(NT):
                        ins = mm(banks[:, w % 2, jt * R * WIN:(jt + 1) * R * WIN],
                                 src_hot[:, k, jt * P:(jt + 1) * P],
                                 dst_hot[:, k, :, :].rearrange("p r i -> p (r i)"),
                                 start=(first and k == 0 and jt == 0), stop=True, skip_group_check=True)
                    ins.then_inc(s_slot, 1)

            def window(w):
                if w >= 2:
                    pe.wait_ge(s_res, w - 1)
                turn(w, True)
                with pe.If(hi[w] > lo[w] + G):
                    with pe.Fori(lo[w] + G, hi[w], G):
                        turn(w, False)
                mm(banks[:, w % 2, 500:501], ident16[:], ident16[:, 0:1], start=False, stop=True,
                   skip_group_check=True).then_inc(s_win, 1)

            def take_bank(u):
                if number[u] >= 3:
                    pe.wait_ge(s_ufree, number[u] - 2)

            def unit(u):
                kind = u[0]
                take_bank(u)
                b = bank(u)
                if kind in ("hT", "h2T"):
                    it = u[1]
                    if kind == "hT":
                        pe.wait_ge(s_y, it + 1)
                        rows = self_sum[:, it, :]
                    else:
                        pe.wait_ge(s_y, NT + it + 1)
                        rows = ybuf[:, it % 2, :]
                    for kt in range(KD):
                        ins = nc.tensor.transpose(b[:, kt * P:(kt + 1) * P], rows[:, kt * P:(kt + 1) * P], ident[:])
                elif kind == "self":
                    _, t, it = u
                    if it == 0:
                        pe.wait_ge(s_wlo, t + 1)
                        pe.wait_ge(s_ufree, NT)
                    ins = gemm(b, hT, it, w_hl[t % 2], 0, D)
                elif kind == "cnt":
                    half = u[1]
                    cols = slice(half * HALF, (half + 1) * HALF)
                    if half == 0:
                        pe.wait_ge(s_adj, NW)
                        pe.wait_ge(s_res, NW)
                        pe.wait_ge(s_keys, 15)
                        pe.wait_ge(s_fill, 19)
                    for it in range(NT):
                        a, z = max(it * P, half * HALF), min((it + 1) * P, (half + 1) * HALF)
                        if a < z:
                            mm(b[0:R + T, a - half * HALF:z - half * HALF], mask6[:, it, :],
                               ident16[:, a - it * P:z - it * P], start=(a == half * HALF), stop=False,
                               skip_group_check=True)
                    with pe.If(widest > EXACT16 // P):
                        for r in range(R):
                            for jt in range(NT):
                                mm(b[0:R + T, 0:HALF], sel6[:, r, :], adjT_res[:, jt, r, cols], start=False,
                                   stop=False, skip_group_check=True)
                    for r in range(R):
                        for jt in range(NT):
                            ins = mm(b[0:R + T, 0:HALF], sel6[:, r, :], adjT[:, jt, r, cols], start=False,
                                     stop=(r == R - 1 and jt == NT - 1), skip_group_check=True)
                elif kind == "z":
                    _, r, dt, half = u
                    cols = slice(half * HALF, (half + 1) * HALF)
                    if (r, dt, half) == (0, 0, 0):
                        pe.wait_ge(s_h16lo, NT)
                    feats = slice(dt * P, (dt + 1) * P)
                    pairs = [(p, jt) for jt in range(NT) for p in range(2)]

                    def add(adj, pick, start, stop):
                        for n, (p, jt) in enumerate(pick):
                            ins = mm(b[:, 0:HALF], h16[:, p, jt, feats], adj[:, jt, r, cols],
                                     start=(start and n == 0), stop=(stop and n == len(pick) - 1),
                                     skip_group_check=True)
                        return ins
                    add(adjT, pairs[:-1], True, False)
                    with pe.If(widest > EXACT16 // P):
                        add(adjT_res, pairs, False, False)
                    ins = add(adjT, pairs[-1:], False, True)
                elif kind == "m":
                    _, it, part = u
                    tiles = range(4) if part == 0 else range(4, NT)
                    items = [(r, jt) for jt in tiles for r in range(R)]

                    def add(adj, pick, start, stop):
                        for n, (r, jt) in enumerate(pick):
                            rows = (jt - tiles[0]) * P
                            ins = mm(b[:, rows:rows + P], adj[:, jt, r, it * P:(it + 1) * P], ident16[:],
                                     start=(start and n == 0), stop=(stop and n == len(pick) - 1),
                                     skip_group_check=True)
                        return ins
                    add(adjT, items[:-1], True, False)
                    with pe.If(widest > EXACT16 // P):
                        add(adjT_res, items, False, False)
                    ins = add(adjT, items[-1:], False, True)
                elif kind == "wt":
                    _, g, kt = u
                    q = NWT + g
                    pe.wait_ge(s_raw[q % 2], 16 * (q // 2 + 1))
                    for o in range(4):
                        ins = nc.tensor.transpose(b[:, o * P:(o + 1) * P], raw[q % 2][:, o, kt * P:(kt + 1) * P],
                                                  ident[:])
                elif kind in ("q", "k"):
                    _, a, half = u
                    o = (0 if kind == "q" else D) + a * P
                    if u == ("q", 0, 0):
                        pe.wait_ge(s_ufree, number[("h2T", NT - 1, 0)] + 1)
                    n = 0
                    for kt in range(KD):
                        for pw, ph in PASSES:
                            ins = mm(b[:, 0:HALF], wqkvT[:, pw, kt, o:o + P],
                                     h2T[:, ph, kt, half * HALF:(half + 1) * HALF],
                                     start=(n == 0), stop=(n == 3 * KD - 1))
                            n += 1
                else:
                    pe.wait_ge(s_ufree, number[("h2T", u[1], 0)] + 1)
                    ins = gemm(b, h2T, u[1], wqkvT, 2 * D, D)
                ins.then_inc(s_unit, 1)

            def gemm(to, lhs, it, weights, c0, cn, start=True):
                n = 0
                for kt in range(KD):
                    for pl, pw in PASSES:
                        ins = mm(to, lhs[:, pl, kt, it * P:(it + 1) * P], weights[:, pw, kt, c0:c0 + cn],
                                 start=(start and n == 0), stop=(n == 3 * KD - 1), skip_group_check=True)
                        n += 1
                return ins

            for w in range(NW):
                window(w)
                unit(ring[w])

            for u in schedule[n_side:]:
                if u[0] == "ln":
                    continue
                if u[0] != "gemm":
                    unit(u)
                    continue
                r = u[1]
                pe.wait_ge(s_wlo, T + r + 1)
                pe.wait_ge(s_ufree, number[("z", r, KD - 1, 1)] + 1)
                for it in range(NT):
                    if r == 0:
                        pe.wait_ge(s_ufree, number[("cnt", 1, 0)] + 1)
                        mm(banks[:, it, :], cnt6[:, it * P:(it + 1) * P], b0[:], start=True, stop=False,
                           skip_group_check=True)
                    ins = gemm(banks[:, it, :], zT[r % 2], it, w_hl[(T + r) % 2], 0, D, start=False)
                    if r == R - 1:
                        ins.then_inc(s_acc, 1)
                if r < R - 1:
                    ins.then_inc(s_gemm, 1)

            for step in attention:
                kind, n = step
                if kind == "score":
                    it, h = divmod(n, H)
                    if n == 0:
                        pe.wait_ge(s_qk, 8 * KD)
                        pe.wait_ge(s_kcp, 2 * KD)
                        pe.wait_ge(s_kcl, 2 * KD)
                    if n >= 2:
                        pe.wait_ge(s_smax, n - 1)
                    for half in range(2):
                        cols = slice(half * HALF, (half + 1) * HALF)
                        for p, k in enumerate((k_hi, k_lo)):
                            ins = mm(banks[:, 2 * (n % 2) + half, 0:HALF], q_st[:, h, it * P:(it + 1) * P],
                                     k[:, h, cols], start=(p == 0), stop=(p == 1))
                    ins.then_inc(s_sc, 1)
                elif kind == "turn":
                    pe.wait_ge(s_exp, n + 1)
                    if n == 0:
                        pe.wait_ge(s_ufree, len(ring))
                    for jt in range(NT):
                        s = n * NT + jt
                        f = s // 4
                        if s % 4 == 0 and f >= 2:
                            pe.wait_ge(s_pta if f % 2 == 0 else s_ptd, f // 2)
                        ins = nc.tensor.transpose(banks[:, 5 + f % 2, (s % 4) * P:(s % 4 + 1) * P],
                                                  p_sb[:, n % 4, jt * P:(jt + 1) * P], ident[:])
                        if s % 4 == 3:
                            ins.then_inc(s_tr, 1)
                elif kind == "pv":
                    it, a = divmod(n, KD)
                    f = ((2 * n + 2) * NT - 1) // 4
                    pe.wait_ge(s_pta, (f + 2) // 2)
                    pe.wait_ge(s_ptd, (f + 1) // 2)
                    if a == 0 and it >= 1:
                        pe.wait_ge(s_msg, it)
                    for jt in range(NT):
                        for hh in range(2):
                            s = ((2 * n + hh) * NT + jt) % (NT * H)
                            h = 2 * a + hh
                            ins = mm(banks[64 * hh:64 * hh + 64, 4, a * P:(a + 1) * P],
                                     v_sb[:, jt, h * DK:(h + 1) * DK], pT[:, s, :],
                                     start=(jt == 0), stop=(jt == NT - 1), skip_group_check=True)
                    ins.then_inc(s_pv, 1)
                elif kind == "norm":
                    pe.wait_ge(s_norm, n + 1)
                    if n >= 1:
                        pe.wait_ge(s_fin, n)
                    for h in range(H):
                        me = 64 * (h % 2)
                        ins = mm(banks[me:me + 64, 7, h // 2 * P:(h // 2 + 1) * P],
                                 norm[:, n % 2, h:h + 1].broadcast_to([P, DK]), ident[:],
                                 start=(h < 2), stop=True, skip_group_check=True)
                    ins.then_inc(s_rb, 1)
                elif kind == "ff":
                    pe.wait_ge(s_mlo, n + 1)
                    pe.wait_ge(s_rsb, n + 1)
                    k = 0
                    for kt in range(KD):
                        for pl, pw in PASSES:
                            ins = mm(banks[:, 7, :], msgT[:, n % 2, pl, kt, :], wffT[:, pw, kt, :],
                                     start=(k == 0), stop=(k == 3 * KD - 1))
                            k += 1
                    ins.then_inc(s_ff, 1)


def load_bounds(eng, nc, bounds, row, nw, last):
    _, values = nc.values_load_multi_w_load_instructions(
        bounds[0:1, row, 0:nw], engines=(eng.engine,), min_val=0, max_val=last,
        skip_runtime_bounds_check_because="the vector engine clamped them")
    return values


INPUTS = ["x", "src", "dst", "edge_type_3", "node_type_3", "L0_gnn_W_rel", "L0_gnn_b_rel", "L0_gnn_W_self",
          "L0_gnn_b_self", "L1_gnn_W_qkv", "L1_gnn_b_qkv", "L1_gnn_W_ff", "L1_gnn_b_ff"]


def kernel(**inputs):
    import numpy as np
    import concourse.bacc as bacc
    from concourse.bass_utils import run_bass_kernel_spmd

    nc = bacc.Bacc("TRN2", target_bir_lowering=False, num_devices=1)
    arrays, args = {}, []
    for name in INPUTS:
        a = np.ascontiguousarray(inputs[name])
        arrays[f"in_{name}_dram"] = a
        args.append(nc.dram_tensor(f"in_{name}_dram", a.shape, mybir.dt.from_np(a.dtype), kind="ExternalInput").ap())
    shape = inputs["x"].shape
    args.append(nc.dram_tensor("out_0_dram", shape, F32, kind="ExternalOutput").ap())
    gnn_kernel(nc, *args)
    result = run_bass_kernel_spmd(nc, [arrays], core_ids=[0])
    return result.results[0]["out_0_dram"]
```

```python
from contextlib import ExitStack

import concourse.bass as bass
from concourse import mybir

F32 = mybir.dt.float32
F32R = mybir.dt.float32r
F16 = mybir.dt.float16
F8 = mybir.dt.float8e4
I32 = mybir.dt.int32
ALU = mybir.AluOpType
ACT = mybir.ActivationFunctionType
AX = mybir.AxisListType

P = 128
BIG = 1.0e30
EPS = 1e-5
EXACT16 = 2048


def gnn_kernel(nc, x_d, src_d, dst_d, etype_d, ntype_d, wrel_d, brel_d, wself_d, bself_d,
               wqkv_d, bqkv_d, wff_d, bff_d, out_d):
    N, D = x_d.shape
    E = src_d.shape[0]
    R = wrel_d.shape[0]
    T = wself_d.shape[0]
    DK = 64
    H = D // DK
    KD = D // P
    NT = -(-N // P)
    NP = NT * P
    LAST = N - (NT - 1) * P
    EL = 125
    EC = E // EL
    WIN = 32
    NW = NP // WIN
    G = 6
    HALF = NP // 2
    NWT = R + T
    SCALE = float(DK) ** -0.5
    NS, NPR = 3, 6
    assert (N, D, E, R, T) == (625, 512, 10000, 3, 3) and EC * EL == E

    with ExitStack() as ctx:
        def sb(name, shape, dt):
            return ctx.enter_context(nc.sbuf_tensor(name, shape, dt))

        def sem(name):
            return ctx.enter_context(nc.semaphore(name))

        xs = sb("xs", [P, NT, D], F32)
        ident = sb("ident", [P, P], F32)
        ident16 = sb("ident16", [P, P], F16)
        b0 = sb("b0", [R + T, D], F32)
        bv_rows = sb("bv_rows", [P, D], F32)
        bff_rows = sb("bff_rows", [P, D], F32)
        ybuf = sb("ybuf", [P, 2, D], F32)
        edges_i = sb("edges_i", [EC, 3, EL], I32)
        edge_keys = sb("edge_keys", [P, 2, 96], F32)
        ntype_i = sb("ntype_i", [NT, P], I32)
        ntype_f = sb("ntype_f", [NT, P], F32)
        type_mask = sb("type_mask", [P, NT, T], F32)
        mask6 = sb("mask6", [P, NT, R + T], F16)
        sel6 = sb("sel6", [P, R, R + T], F16)
        cnt6 = sb("cnt6", [R + T, NP], F32)
        bqkv_r = sb("bqkv_r", [3 * KD, P], F32)
        bqk = sb("bqk", [P, 2 * KD], F32)
        chunk_mm = sb("chunk_mm", [EC, 2], F32)
        win_iota = sb("win_iota", [NW, 2], F32)
        c_iota = sb("c_iota", [NW, 2, EC], F32)
        cover = sb("cover", [NW, 3, EC], F32)
        win_c = sb("win_c", [NW, 4], F32)
        bounds = sb("bounds", [1, 3, 32], I32)
        bounds_f = sb("bounds_f", [1, 4, 32], F32)
        stats = sb("stats", [P, NT, 6], F32)
        mv = sb("mv", [P, 2, NT, 2], F32)
        rstd = sb("rstd", [P, 2, NT, 2], F32)
        warm = sb("warm", [P, 2], F32)
        shift0 = sb("shift0", [P, NT], F32)
        eps_c = sb("eps_c", [P, 1], F32)
        mask_add = sb("mask_add", [P, NT, NP], F32)
        neg_max = sb("neg_max", [P, NT, H], F32)
        denom = sb("denom", [P, NT, H], F32)
        recip = sb("recip", [P, 2, H], F32)
        norm = sb("norm", [P, 2, H], F32)

        Z_BYTES = 2 * KD * NP * 4
        W_BYTES = 2 * KD * D * 4
        RAW_BYTES = KD * D * 4
        ctx.enter_context(nc.sbuf_tensor("arena", [P, 167936 // 4], F32))
        arena0 = nc.sbuf_base - 167936
        at_byte = {}

        def place(name, offset, shape, dt):
            t = nc.alloc_sbuf_tensor_at(name, shape, dt, offset=arena0 + offset)
            return t

        o_z1, o_z0 = 0, Z_BYTES
        o_w = 2 * Z_BYTES
        o_raw = o_w + 2 * W_BYTES
        o_r4 = o_raw + 2 * RAW_BYTES + 2048
        o_ss = o_r4 + 4 * 4 * D * 2 * 4
        hT = place("hT", o_z1, [P, 2, KD, NP], F32R)
        zT = [place("zT_even", o_z0, [P, 2, KD, NP], F32R), place("zT_odd", o_z1, [P, 2, KD, NP], F32R)]
        h2T = place("h2T", o_z1, [P, 2, KD, NP], F32R)
        w_hl = [place(f"w_hl{i}", o_w + i * W_BYTES, [P, 2, KD, D], F32R) for i in range(2)]
        raw = [place(f"raw{i}", o_raw + i * RAW_BYTES, [P, KD, D], F32) for i in range(2)]
        h16 = place("h16", o_r4, [P, 2, NT, D], F16)
        adjT = place("adjT", o_r4 + 10240, [P, NT, R, NP], F16)
        adjT_res = place("adjT_res", o_r4 + 29440, [P, NT, R, NP], F8)
        src_hot = place("src_hot", o_r4 + 39040, [P, 2, G, NP], F16)
        dst_hot = place("dst_hot", o_r4 + 54400, [P, 2, G, R * WIN], F16)
        iota = place("iota", o_r4 + 56704, [P, R, NP], F16)
        mcount = place("mcount", o_r4 + 39040, [P, 2, 512], F32)
        edges_f = place("edges_f", o_r4 + 60544, [EC, 2, EL], F32)
        mlog = place("mlog", o_r4 + 43136, [P, 2, 512], F32)
        self_sum = place("self_sum", o_ss, [P, NT, D], F32)
        in0 = place("in0", o_z0, [P, NT, D], F32)
        wqkvT = place("wqkvT", o_r4, [P, 2, KD, 3 * D], F32R)
        wffT = place("wffT", o_r4 + 49152, [P, 2, KD, D], F32R)
        q_st = place("q_st", o_z0, [P, H, NP], F32R)
        k_hi = place("k_hi", o_z0 + 20480, [P, H, NP], F32R)
        k_lo = place("k_lo", o_z0 + 40960, [P, H, NP], F32R)
        v_sb = place("v_sb", o_z0 + 61440, [P, NT, D], F32)
        qk_f = place("qk_f", o_ss, [P, 2, NP], F32)
        s_sb = place("s_sb", o_r4, [P, NS, NP], F32)
        p_sb = place("p_sb", o_r4 + 7680, [P, NPR, NP], F32)
        pT = place("pT", o_z1, [P, NT * H, P], F32)
        msg_f = place("msg_f", o_r4 + 23040, [P, KD, P], F32)
        r_sb = place("r_sb", o_r4 + 25088, [P, KD, P], F32)
        msgT = place("msgT", o_r4 + 27136, [P, 2, 2, KD, P], F32R)

        banks = ctx.enter_context(nc.psum_tensor("banks", [P, 8, 512], F32))

        s_fill = sem("s_fill")
        s_edges = sem("s_edges")
        s_nodes = sem("s_nodes")
        s_x = sem("s_x")
        s_bias = sem("s_bias")
        s_raw = [sem("s_raw0"), sem("s_raw1")]
        s_keys = sem("s_keys")
        s_prep = sem("s_prep")
        s_chain = sem("s_chain")
        s_src = [sem("s_src0"), sem("s_src1")]
        s_dst = [sem("s_dst0"), sem("s_dst1")]
        s_slot = [sem("s_slot0"), sem("s_slot1")]
        s_win = sem("s_win")
        s_adj = sem("s_adj")
        s_res = sem("s_res")
        s_var = sem("s_var")
        s_norm0 = sem("s_norm0")
        s_std = sem("s_std")
        s_y0 = sem("s_y0")
        s_y = sem("s_y")
        s_h16hi = sem("s_h16hi")
        s_whi = sem("s_whi")
        s_wlo = sem("s_wlo")
        s_unit = sem("s_unit")
        s_uhi = sem("s_uhi")
        s_ufree = sem("s_ufree")
        s_gemm = sem("s_gemm")
        s_acc = sem("s_acc")
        s_mc = sem("s_mc")
        s_ln = sem("s_ln")
        s_h16lo = sem("s_h16lo")
        s_mask = sem("s_mask")
        s_qk = sem("s_qk")
        s_kcp = sem("s_kcp")
        s_kcl = sem("s_kcl")
        s_sc = sem("s_sc")
        s_smax = sem("s_smax")
        s_exp = sem("s_exp")
        s_tr = sem("s_tr")
        s_pta = sem("s_pta")
        s_ptd = sem("s_ptd")
        s_pv = sem("s_pv")
        s_norm = sem("s_norm")
        s_rb = sem("s_rb")
        s_rsb = sem("s_rsb")
        s_msg = sem("s_msg")
        s_mhi = sem("s_mhi")
        s_mlo = sem("s_mlo")
        s_ff = sem("s_ff")
        s_xb = sem("s_xb")
        s_x1 = sem("s_x1")
        s_fin = sem("s_fin")
        s_out = [sem("s_out0"), sem("s_out1")]

        side = {w: [] for w in range(NW)}
        side[1] = [("hT", 0, 0), ("hT", 1, 0)]
        side[2] = [("hT", 2, 0), ("hT", 3, 0)]
        side[3] = [("hT", 4, 0), ("self", 0, 0)]
        for n in range(1, T * NT):
            side[3 + n].append(("self", n // NT, n % NT))

        def z_units(r):
            return [("z", r, dt, half) for dt in range(KD) for half in range(2)]

        schedule = [("cnt", half, 0) for half in range(2)] + z_units(0) + z_units(1)
        for it in range(NT):
            schedule += [("gemm", 0, it), ("m", it, 0), ("m", it, 1)]
        schedule += z_units(2)
        wt_units = [("wt", g, kt) for g in range(3) for kt in range(KD)]
        for it in range(NT):
            schedule += [("gemm", 1, it)] + wt_units[3 * it:3 * it + 3]
        schedule += [("wt", 3, 0), ("wt", 3, 1)]
        for it in range(NT):
            schedule.append(("gemm", 2, it))
            if it >= 2:
                schedule.append(("h2T", it - 2, 0))
            schedule.append(("ln", it))
            if it == 0:
                schedule += [("wt", 3, 2), ("wt", 3, 3)]
        schedule += [("v", 0, 0), ("v", 1, 0), ("h2T", 3, 0), ("v", 2, 0), ("h2T", 4, 0), ("v", 3, 0), ("v", 4, 0)]
        schedule += [("k", a, half) for a in range(KD) for half in range(2)]
        schedule += [("q", a, half) for a in range(KD) for half in range(2)]
        ring = [u for w in range(NW) for u in side[w]] + [u for u in schedule if u[0] not in ("gemm", "ln")]
        number = {u: n for n, u in enumerate(ring)}

        def bank(u):
            return banks[:, 5 + number[u] % 3, :]

        def used_weights(eng, q):
            if q < T:
                eng.wait_ge(s_unit, number[("self", q, NT - 1)] + 1)
            else:
                eng.wait_ge(s_gemm, q - T + 1)

        act_units = [u for u in ring if u[0] in ("hT", "z", "wt", "h2T", "q", "k")]
        act_done = {u: n + 1 for n, u in enumerate(act_units)}
        m_units = [u for u in ring if u[0] == "m"]

        def m_cols(part):
            return (0, 4 * P) if part == 0 else (4 * P, P)

        attention = []
        LAG = 3
        for m in range(NT * H + 8):
            if m < NT * H:
                attention += [("score", m), ("smax", m)]
            if 0 <= m - LAG < NT * H:
                attention.append(("turn", m - LAG))
                attention += [("fill", f) for f in range(NT * NT * H // 4) if (4 * f + 3) // NT == m - LAG]
            if m < NT * H:
                attention.append(("exp", m))
            if m >= 10 and (m - 10) % H == 0 and (m - 10) // H < NT:
                attention.append(("norm", (m - 10) // H))
            if m >= 11 and (m - 11) % H == 0 and (m - 11) // H < NT:
                attention.append(("rb", (m - 11) // H))
            if m >= LAG + 3 and (m - LAG - 3) % 2 == 0 and (m - LAG - 3) // 2 < NT * KD:
                attention.append(("pv", (m - LAG - 3) // 2))
            if m >= LAG + 10 and (m - LAG - 10) % H == 0:
                attention.append(("msg", (m - LAG - 10) // H))
            if m >= LAG + 11 and (m - LAG - 11) % H == 0:
                attention += [("ff", (m - LAG - 11) // H), ("out", (m - LAG - 11) // H)]

        WINDOW_CHUNKS, BOUNDS, EDGE_KEYS, MASKS, BIASES = 6, 9, 10, 14, 16

        block = ctx.enter_context(nc.Block())

        @block.sync
        def _(sp):
            for k, arr in ((1, dst_d), (2, etype_d), (0, src_d)):
                sp.dma_start(edges_i[:, k, :], arr.rearrange("(c p) -> c p", p=EL)).then_inc(s_edges, 16)
            sp.wait_ge(s_fill, 2)
            sp.dma_start(xs[:, 0:NT - 1, :], x_d[0:(NT - 1) * P, :].rearrange("(t p) d -> p t d", p=P)
                         ).then_inc(s_x, 16)
            sp.dma_start(xs[0:LAST, NT - 1, :], x_d[(NT - 1) * P:N, :]).then_inc(s_x, 16)
            for q in range(NWT + 4):
                if q >= 2 and q - 2 < NWT:
                    sp.wait_ge(s_wlo, KD * (q - 1))
                elif q >= 2:
                    sp.wait_ge(s_unit, number[("wt", q - 2 - NWT, KD - 1)] + 1)
                if q < T:
                    w = wself_d[q].rearrange("(k p) n -> p k n", p=P)
                elif q < NWT:
                    w = wrel_d[q - T].rearrange("(k p) n -> p k n", p=P)
                elif q < NWT + 3:
                    w = wqkv_d[(q - NWT) * D:(q - NWT + 1) * D, :].rearrange("(k p) n -> p k n", p=P)
                else:
                    w = wff_d.rearrange("(k p) n -> p k n", p=P)
                sp.dma_start(raw[q % 2][:], w).then_inc(s_raw[q % 2], 16)
            for it in range(NT):
                rows = P if it < NT - 1 else LAST
                sp.wait_ge(s_fin, it + 1)
                sp.dma_start(out_d[it * P:it * P + rows, :], ybuf[0:rows, it % 2, :]).then_inc(s_out[it % 2], 16)
            sp.wait_ge(s_out[0], 16 * -(-NT // 2))
            sp.wait_ge(s_out[1], 16 * (NT // 2))

        @block.gpsimd
        def _(pool):
            nc.gpsimd.memset(ntype_i[:], 0).then_inc(s_fill, 1)
            nc.gpsimd.memset(xs[:, NT - 1, :], 0.0).then_inc(s_fill, 1)
            nc.gpsimd.memset(ident[:], 0.0).then_inc(s_fill, 1)
            pool.wait_ge(s_fill, 3)
            nc.gpsimd.affine_select(out=ident[:], in_=ident[:], compare_op=ALU.not_equal, fill=1.0, base=0,
                                    pattern=[[-1, P]], channel_multiplier=1).then_inc(s_fill, 1)
            nc.gpsimd.iota(win_iota[:], [[WIN, 2]], base=0, channel_multiplier=WIN,
                           allow_small_or_imprecise_dtypes=True).then_inc(s_fill, 1)
            nc.gpsimd.iota(c_iota[:, 0, :], [[1, EC]], base=1, channel_multiplier=0,
                           allow_small_or_imprecise_dtypes=True).then_inc(s_fill, 1)
            nc.gpsimd.iota(c_iota[:, 1, :], [[-1, EC]], base=EC, channel_multiplier=0,
                           allow_small_or_imprecise_dtypes=True).then_inc(s_fill, 1)
            nc.gpsimd.memset(edge_keys[:], -1.0).then_inc(s_fill, 1)
            nc.gpsimd.iota(iota[:], [[1, R * NP]], base=0, channel_multiplier=0,
                           allow_small_or_imprecise_dtypes=True).then_inc(s_fill, 1)
            pool.wait_ge(s_fill, 4)
            nc.gpsimd.tensor_copy(ident16[:], ident[:]).then_inc(s_fill, 1)
            nc.gpsimd.memset(sel6[:], 0.0).then_inc(s_fill, 1)
            nc.gpsimd.memset(mask6[:], 0.0).then_inc(s_fill, 1)
            nc.gpsimd.memset(eps_c[:], EPS).then_inc(s_fill, 1)
            pool.wait_ge(s_fill, 11)
            for r in range(R):
                nc.gpsimd.memset(sel6[:, r, r:r + 1], 1.0).then_inc(s_fill, 1)
            def weights_lo(q, kt):
                pool.wait_ge(s_whi, q + 1)
                nc.gpsimd.tensor_tensor(w_hl[q % 2][:, 1, kt], raw[q % 2][:, kt],
                                        w_hl[q % 2][:, 0, kt].bitcast(F32), ALU.subtract).then_inc(s_wlo, 1)

            pieces = {0: [(0, 0), (0, 1)], 1: [(0, 2), (0, 3)]}
            for q, w0 in ((1, 4), (2, 9), (3, 14)):
                for kt in range(KD):
                    pieces[w0 + kt] = [(q, kt)]
            for w in range(NW):
                for q, kt in pieces.get(w, []):
                    weights_lo(q, kt)
                if 10 <= w < 10 + NT:
                    it = w - 10
                    pool.wait_ge(s_h16hi, it + 1)
                    nc.gpsimd.tensor_tensor(h16[:, 1, it, :], in0[:, it, :], h16[:, 0, it, :], ALU.subtract
                                            ).then_inc(s_h16lo, 1)
            for kt in range(KD):
                weights_lo(4, kt)
            for n, u in enumerate(m_units):
                _, it, part = u
                c0, cn = m_cols(part)
                pool.wait_ge(s_ln, n + 1)
                pool.wait_ge(s_ufree, number[u] + 1)
                nc.gpsimd.tensor_tensor(mask_add[:, it, c0:c0 + cn], mask_add[:, it, c0:c0 + cn],
                                        mlog[:, n % 2, 0:cn], ALU.subtract).then_inc(s_mask, 1)
            for kt in range(KD):
                weights_lo(5, kt)
            for it in range(NT):
                pool.wait_ge(s_bias, 80)
                pool.wait_ge(s_y, it + 1)
                nc.gpsimd.tensor_tensor(xs[:, it, :], xs[:, it, :], bff_rows[:], ALU.add).then_inc(s_xb, 1)
            pool.wait_ge(s_xb, NT)
            for a in range(KD):
                pool.wait_ge(s_qk, 4 * (a + 1))
                for hh in range(2):
                    me, other = 64 * hh, 64 - 64 * hh
                    if a or hh:
                        pool.wait_ge(s_kcl, 2 * a + hh)
                    nc.gpsimd.tensor_copy(k_lo[other:other + 64, 2 * a + hh, :],
                                          k_lo[me:me + 64, 2 * a + hh, :].bitcast(F32)).then_inc(s_kcl, 1)
            for it in range(NT):
                if it == 0:
                    pool.wait_ge(s_kcl, 2 * KD)
                pool.wait_ge(s_mhi, it + 1)
                nc.gpsimd.tensor_tensor(msgT[:, it % 2, 1], msg_f[:], msgT[:, it % 2, 0].bitcast(F32),
                                        ALU.subtract).then_inc(s_mlo, 1)

        @block.scalar
        def _(act):
            act.wait_ge(s_fill, 1)
            act.dma_start(ntype_i[0:NT - 1, :], ntype_d[0:(NT - 1) * P].rearrange("(t p) -> t p", p=P)
                          ).then_inc(s_nodes, 16)
            act.dma_start(ntype_i[NT - 1:NT, 0:LAST], ntype_d[(NT - 1) * P:N].rearrange("(t p) -> t p", t=1)
                          ).then_inc(s_nodes, 16)
            act.dma_start(b0[0:R, :], brel_d).then_inc(s_bias, 16)
            act.dma_start(b0[R:R + T, :], bself_d).then_inc(s_bias, 16)
            act.dma_start(bqkv_r[:], bqkv_d.rearrange("(o p) -> o p", p=P)).then_inc(s_bias, 16)
            act.dma_start(bv_rows[:], bqkv_d[2 * D:3 * D].partition_broadcast(P)).then_inc(s_bias, 16)
            act.dma_start(bff_rows[:], bff_d.partition_broadcast(P)).then_inc(s_bias, 16)

            def weights_hi(q):
                act.wait_ge(s_raw[q % 2], 16 * (q // 2 + 1))
                if q >= 2:
                    used_weights(act, q - 2)
                nc.scalar.activation(w_hl[q % 2][:, 0], raw[q % 2][:], ACT.Copy).then_inc(s_whi, 1)

            def standard_deviation(layer, t0, t1, count):
                act.wait_ge(s_var, count)
                nc.scalar.activation(rstd[:, layer, t0:t1, 0], mv[:, layer, t0:t1, 1], ACT.Sqrt,
                                     bias=eps_c[:]).then_inc(s_std, 1)

            def store_window(w):
                act.wait_ge(s_win, w + 1)
                nc.scalar.activation(adjT[:, :, :, w * WIN:(w + 1) * WIN],
                                     banks[:, w % 2, 0:NT * R * WIN].rearrange("p (t r i) -> p t r i", t=NT, r=R),
                                     ACT.Copy).then_inc(s_adj, 1)

            act.wait_ge(s_fill, 16)
            nc.scalar.activation(warm[:, 0:1], eps_c[:], ACT.Sqrt)
            weights_hi(0)
            standard_deviation(0, 0, NT, 1)
            act.wait_ge(s_norm0, 1)

            def rows0(it):
                nc.scalar.activation(in0[:, it, :], xs[:, it, :], ACT.Relu, bias=shift0[:, it:it + 1],
                                     scale=rstd[:, 0, it, 1:2]).then_inc(s_y0, 1)

            def h16_hi(it):
                act.wait_ge(s_y0, it + 1)
                nc.scalar.activation(h16[:, 0, it, :], in0[:, it, :], ACT.Copy).then_inc(s_h16hi, 1)

            for it in range(NT):
                rows0(it)

            def unit_part(u):
                kind = u[0]
                if kind not in ("hT", "z", "wt", "h2T", "q", "k"):
                    return
                act.wait_ge(s_unit, number[u] + 1)
                if kind == "hT":
                    it = u[1]
                    ins = nc.scalar.activation(hT[:, 0, :, it * P:(it + 1) * P],
                                               bank(u).rearrange("p (k i) -> p k i", k=KD), ACT.Copy)
                elif kind == "h2T":
                    it = u[1]
                    ins = nc.scalar.activation(h2T[:, 0, :, it * P:(it + 1) * P],
                                               bank(u).rearrange("p (k i) -> p k i", k=KD), ACT.Relu)
                elif kind == "z":
                    _, r, dt, half = u
                    if u == ("z", 0, 0, 0):
                        act.wait_ge(s_h16lo, NT)
                    ins = nc.scalar.activation(zT[r % 2][:, 0, dt, half * HALF:(half + 1) * HALF],
                                               bank(u)[:, 0:HALF], ACT.Copy)
                elif kind == "wt":
                    _, g, kt = u
                    if u == ("wt", 0, 0):
                        act.wait_ge(s_mask, len(m_units))
                    to = wqkvT[:, 0, kt, g * D:(g + 1) * D] if g < 3 else wffT[:, 0, kt, :]
                    ins = nc.scalar.activation(to, bank(u), ACT.Copy)
                else:
                    _, a, half = u
                    n = a if kind == "k" else KD + a
                    if n == 0:
                        act.wait_ge(s_keys, BIASES)
                    if n >= 2:
                        act.wait_ge(s_qk, 4 * (n - 1))
                    ins = nc.scalar.activation(qk_f[:, n % 2, half * HALF:(half + 1) * HALF], bank(u)[:, 0:HALF],
                                               ACT.Identity, bias=bqk[:, n:n + 1],
                                               scale=-SCALE if kind == "q" else 1.0)
                ins.then_inc(s_uhi, 1)

            w_at = {4: 1, 9: 2, 14: 3, 19: 4}
            for w in range(NW):
                if w >= 1:
                    for u in side[w - 1]:
                        unit_part(u)
                store_window(w)
                if w in w_at:
                    weights_hi(w_at[w])
                if 10 <= w < 10 + NT:
                    h16_hi(w - 10)
            n_ln = 0
            for u in schedule:
                if u == ("z", 2, 0, 0):
                    weights_hi(5)
                if u[0] == "m":
                    cn = m_cols(u[2])[1]
                    act.wait_ge(s_mc, n_ln + 1)
                    if n_ln >= 2:
                        act.wait_ge(s_mask, n_ln - 1)
                    nc.scalar.activation(mlog[:, n_ln % 2, 0:cn], mcount[:, n_ln % 2, 0:cn], ACT.Ln
                                         ).then_inc(s_ln, 1)
                    n_ln += 1
                    continue
                if u[0] == "ln":
                    standard_deviation(1, u[1], u[1] + 1, 2 + u[1])
                    if u[1] == NT - 1:
                        nc.scalar.activation(warm[:, 1:2], eps_c[:], ACT.Exp)
                    continue
                if u[0] == "gemm":
                    continue
                unit_part(u)
                if u[0] == "k" and u[2] == 1:
                    a = u[1]
                    for hh in range(2):
                        me, other = 64 * hh, 64 - 64 * hh
                        act.wait_ge(s_qk, 4 * a + hh + 1)
                        nc.scalar.activation(k_hi[other:other + 64, 2 * a + hh, :],
                                             k_hi[me:me + 64, 2 * a + hh, :].bitcast(F32), ACT.Copy
                                             ).then_inc(s_kcp, 1)

            for step in attention:
                kind, n = step
                if kind == "exp":
                    it, h = divmod(n, H)
                    act.wait_ge(s_smax, n + 1)
                    if n >= NPR:
                        act.wait_ge(s_tr, -(-(n - NPR + 1) * NT // 4))
                    nc.scalar.activation(p_sb[:, n % NPR, :], s_sb[:, n % NS, :], ACT.Exp, scale=-1.0,
                                         bias=neg_max[:, it, h:h + 1],
                                         accum_out=denom[:, it, h:h + 1]).then_inc(s_exp, 1)
                elif kind == "fill" and n % 2 == 0:
                    act.wait_ge(s_tr, n + 1)
                    if 4 * n + 3 >= NT * H:
                        act.wait_ge(s_pv, (4 * n + 3 - NT * H) // (2 * NT) + 1)
                    nc.scalar.activation(pT[:, 4 * n % (NT * H):4 * n % (NT * H) + 4, :],
                                         banks[:, 5 + n % 2, :].rearrange("p (s i) -> p s i", s=4), ACT.Copy
                                         ).then_inc(s_pta, 1)
                elif kind == "rb":
                    act.wait_ge(s_rb, n + 1)
                    if n >= 1:
                        act.wait_ge(s_msg, n)
                    nc.scalar.activation(r_sb[:], banks[:, 7, :].rearrange("p (a i) -> p a i", a=KD), ACT.Copy
                                         ).then_inc(s_rsb, 1)
                elif kind == "msg":
                    act.wait_ge(s_msg, n + 1)
                    if n >= 2:
                        act.wait_ge(s_ff, n - 1)
                    nc.scalar.activation(msgT[:, n % 2, 0], msg_f[:], ACT.Copy).then_inc(s_mhi, 1)

        @block.vector
        def _(dve):
            links = [0]

            def chain(ins):
                links[0] += 1
                ins.then_inc(s_chain, 1)
                dve.wait_ge(s_chain, links[0])

            dve.wait_ge(s_edges, 48)
            nc.vector.tensor_reduce(chunk_mm[:, 0:1], edges_i[:, 1, :], AX.X, ALU.min).then_inc(s_keys, 1)
            nc.vector.tensor_reduce(chunk_mm[:, 1:2], edges_i[:, 1, :], AX.X, ALU.max).then_inc(s_keys, 1)
            nc.vector.tensor_copy(edges_f[:, 0, :], edges_i[:, 0, :]).then_inc(s_keys, 1)
            nc.vector.scalar_tensor_tensor(out=edges_f[:, 1, :], in0=edges_i[:, 2, :], scalar=float(NP),
                                           in1=edges_i[:, 1, :], op0=ALU.mult, op1=ALU.add).then_inc(s_keys, 1)
            dve.wait_ge(s_nodes, 32)
            nc.vector.tensor_copy(ntype_f[:], ntype_i[:]).then_inc(s_keys, 1)

            def statistics(layer, it):
                chain(nc.vector.bn_stats(stats[:, it, :], xs[:, it, :]))
                return nc.vector.bn_aggr(mv[:, layer, it, :], stats[:, it, :])

            def normalise(layer, it, to):
                nc.vector.tensor_scalar(to, xs[:, it, :], mv[:, layer, it, 0:1], rstd[:, layer, it, 1:2],
                                        ALU.subtract, ALU.mult).then_inc(s_y, 1)

            dve.wait_ge(s_fill, 8)
            dve.wait_ge(s_prep, 1)
            low = banks[0:NW, 2, 0:EC]
            high = banks[0:NW, 2, EC:2 * EC]
            chain(nc.vector.tensor_scalar(cover[:, 0, :], low, win_iota[:, 1:2], None, ALU.is_lt))
            chain(nc.vector.scalar_tensor_tensor(out=cover[:, 1, :], in0=high, scalar=win_iota[:, 0:1],
                                                 in1=cover[:, 0, :], op0=ALU.is_ge, op1=ALU.mult))
            chain(nc.vector.tensor_tensor_reduce(cover[:, 2, :], cover[:, 1, :], c_iota[:, 0, :], 1.0, 0.0,
                                                 ALU.mult, ALU.max, win_c[:, 1:2]))
            chain(nc.vector.tensor_tensor_reduce(cover[:, 2, :], cover[:, 1, :], c_iota[:, 1, :], 1.0, 0.0,
                                                 ALU.mult, ALU.max, win_c[:, 0:1]))
            chain(nc.vector.tensor_scalar(win_c[:, 0:1], win_c[:, 0:1], -1.0, float(EC), ALU.mult, ALU.add))
            nc.vector.tensor_scalar(win_c[:, 2:3], win_c[:, 0:1], float(EC - 1), None, ALU.min
                                    ).then_inc(s_keys, 1)
            dve.wait_ge(s_x, 32)
            statistics(0, 0)
            dve.wait_ge(s_prep, 2)
            brow = banks[0:1, 3, 0:2 * NW]
            chain(nc.vector.tensor_copy(bounds_f[:, 0:2, 0:NW], brow.rearrange("p (b w) -> p b w", b=2)))
            chain(nc.vector.scalar_tensor_tensor(out=bounds_f[:, 2, 0:NW], in0=bounds_f[:, 0, 0:NW], scalar=1.0,
                                                 in1=bounds_f[:, 1, 0:NW], op0=ALU.add, op1=ALU.max))
            chain(nc.vector.tensor_tensor(bounds_f[:, 3, 0:NW], bounds_f[:, 2, 0:NW], bounds_f[:, 0, 0:NW],
                                          ALU.subtract))
            chain(nc.vector.tensor_reduce(bounds_f[:, 3, 31:32], bounds_f[:, 3, 0:NW], AX.X, ALU.max))
            nc.vector.tensor_copy(bounds[:, 0, 0:NW], bounds_f[:, 0, 0:NW]).then_inc(s_keys, 1)
            nc.vector.tensor_copy(bounds[:, 1, 0:NW], bounds_f[:, 2, 0:NW]).then_inc(s_keys, 1)
            nc.vector.tensor_copy(bounds[:, 2, 0:1], bounds_f[:, 3, 31:32]).then_inc(s_keys, 1)
            dve.wait_ge(s_prep, 3)
            nc.vector.tensor_copy(edge_keys[0:EL, :, 0:EC], banks[0:EL, 4, 0:2 * EC].rearrange("p (k c) -> p k c", k=2)
                                  ).then_inc(s_keys, 1)
            for it in range(1, NT):
                ins = nc.vector.bn_stats(stats[:, it, :], xs[:, it, :])
            links[0] += 1
            ins.then_inc(s_chain, 1)
            dve.wait_ge(s_keys, BOUNDS)
            lo = load_bounds(dve, nc, bounds, 0, NW, EC)
            hi = load_bounds(dve, nc, bounds, 1, NW, EC)
            widest = dve.value_load(bounds[0:1, 2, 0:1], min_val=1, max_val=EC)
            asked = [dve.alloc_register(name=f"asked_dve_{i}") for i in range(2)]
            for par in range(2):
                dve.reg_mov(asked[par], G // 2)

            dve.wait_ge(s_chain, links[0])
            for it in range(1, NT):
                ins = nc.vector.bn_aggr(mv[:, 0, it, :], stats[:, it, :])
            ins.then_inc(s_var, 1)

            def masks():
                for t in range(T):
                    nc.vector.tensor_scalar(type_mask[:, :, t], banks[:, 4, 160:160 + NT], float(t), None,
                                            ALU.is_equal).then_inc(s_keys, 1)
                dve.wait_ge(s_fill, 16)
                dve.wait_ge(s_keys, MASKS - 1)
                nc.vector.tensor_copy(mask6[:, :, R:R + T], type_mask[:]).then_inc(s_keys, 1)

            def biases():
                dve.wait_ge(s_prep, 4)
                nc.vector.tensor_copy(bqk[:, 0:KD], banks[:, 2, 176 + KD:176 + 2 * KD]).then_inc(s_keys, 1)
                nc.vector.tensor_scalar(bqk[:, KD:2 * KD], banks[:, 2, 176:176 + KD], -SCALE, None, ALU.mult
                                        ).then_inc(s_keys, 1)

            def factors0():
                dve.wait_ge(s_std, 1)
                chain(nc.vector.reciprocal(rstd[:, 0, :, 1], rstd[:, 0, :, 0]))
                nc.vector.scalar_tensor_tensor(out=shift0[:], in0=mv[:, 0, :, 0], scalar=-1.0, in1=rstd[:, 0, :, 1],
                                               op0=ALU.mult, op1=ALU.mult).then_inc(s_norm0, 1)

            def one_hots(w):
                par = w % 2
                with dve.Fori(lo[w], hi[w], G) as c:
                    for k in range(G):
                        if k % (G // 2) == 0:
                            dve.wait_ge(s_slot[par], dve.snap(asked[par], min_val=1, max_val=1 << 20))
                            dve.reg_add(asked[par], asked[par], G // 2)
                            g, n = slice(k, k + G // 2), G // 2
                            nc.vector.tensor_tensor(
                                dst_hot[:, par, g].rearrange("p g (r i) -> p g r i", r=R),
                                iota[:, :, w * WIN:(w + 1) * WIN].unsqueeze(1).broadcast_to([P, n, R, WIN]),
                                edge_keys[:, 1, bass.ds(c + k, n)].unsqueeze(2).unsqueeze(3)
                                .broadcast_to([P, n, R, WIN]), ALU.is_equal).then_inc(s_dst[par], n)
                        nc.vector.tensor_scalar(src_hot[:, par, k, :], iota[:, 0, :],
                                                edge_keys[:, 0, bass.ds(c + k, 1)], None, ALU.is_equal
                                                ).then_inc(s_src[par], 1)

            def residual(w):
                dve.wait_ge(s_adj, w + 1)
                with dve.If(widest > EXACT16 // EL):
                    nc.vector.tensor_tensor(
                        adjT_res[:, :, :, w * WIN:(w + 1) * WIN],
                        banks[:, w % 2, 0:NT * R * WIN].rearrange("p (t r i) -> p t r i", t=NT, r=R),
                        adjT[:, :, :, w * WIN:(w + 1) * WIN], ALU.subtract, saturate=False)
                nc.vector.engine_nop().then_inc(s_res, 1)

            def unit_part(u):
                kind = u[0]
                b = bank(u)
                dve.wait_ge(s_unit, number[u] + 1)
                if u in act_done:
                    dve.wait_ge(s_uhi, act_done[u])
                if kind in ("hT", "h2T"):
                    it = u[1]
                    to = hT if kind == "hT" else h2T
                    nc.vector.scalar_tensor_tensor(
                        out=to[:, 1, :, it * P:(it + 1) * P], in0=b.rearrange("p (k i) -> p k i", k=KD), scalar=0.0,
                        in1=to[:, 0, :, it * P:(it + 1) * P].bitcast(F32), op0=ALU.max, op1=ALU.subtract
                    ).then_inc(s_ufree, 1)
                elif kind == "self":
                    _, t, it = u
                    m = type_mask[:, it, t:t + 1]
                    if t == 0:
                        nc.vector.tensor_scalar(self_sum[:, it, :], b, m, None, ALU.mult).then_inc(s_ufree, 1)
                    else:
                        dve.wait_ge(s_ufree, number[("self", t - 1, it)] + 1)
                        nc.vector.scalar_tensor_tensor(out=self_sum[:, it, :], in0=b, scalar=m,
                                                       in1=self_sum[:, it, :], op0=ALU.mult, op1=ALU.add
                                                       ).then_inc(s_ufree, 1)
                elif kind == "cnt":
                    half = u[1]
                    nc.vector.tensor_copy(cnt6[:, half * HALF:(half + 1) * HALF], b[0:R + T, 0:HALF]
                                          ).then_inc(s_ufree, 1)
                elif kind == "z":
                    _, r, dt, half = u
                    cols = slice(half * HALF, (half + 1) * HALF)
                    nc.vector.tensor_tensor(zT[r % 2][:, 1, dt, cols], b[:, 0:HALF],
                                            zT[r % 2][:, 0, dt, cols].bitcast(F32), ALU.subtract
                                            ).then_inc(s_ufree, 1)
                elif kind == "wt":
                    _, g, kt = u
                    to = (lambda part: wqkvT[:, part, kt, g * D:(g + 1) * D]) if g < 3 else \
                         (lambda part: wffT[:, part, kt, :])
                    nc.vector.tensor_tensor(to(1), b, to(0).bitcast(F32), ALU.subtract).then_inc(s_ufree, 1)
                elif kind == "m":
                    _, it, part = u
                    n = m_units.index(u)
                    c0, cn = m_cols(part)
                    if n >= 2:
                        dve.wait_ge(s_ln, n - 1)
                    nc.vector.tensor_scalar(mcount[:, n % 2, 0:cn], b[:, 0:cn], 1.0, None, ALU.max
                                            ).then_inc(s_mc, 1)
                    nc.vector.tensor_scalar(mask_add[:, it, c0:c0 + cn], b[:, 0:cn], 0.0, BIG,
                                            ALU.is_equal, ALU.mult).then_inc(s_ufree, 1)
                elif kind == "v":
                    jt = u[1]
                    dve.wait_ge(s_bias, 80)
                    nc.vector.tensor_tensor(v_sb[:, jt, :], b, bv_rows[:], ALU.add).then_inc(s_ufree, 1)
                elif kind == "q":
                    nc.vector.engine_nop().then_inc(s_ufree, 1)
                    if u[2] == 1:
                        split_q(u[1])
                else:
                    nc.vector.engine_nop().then_inc(s_ufree, 1)
                    if u[2] == 1:
                        split_k(u[1])

            def split_q(a):
                f = qk_f[:, (KD + a) % 2, :]
                for hh in range(2):
                    me = 64 * hh
                    nc.vector.tensor_copy(q_st[me:me + 64, 2 * a + hh, :], f[me:me + 64]).then_inc(s_qk, 1)
                for hh in range(2):
                    me, other = 64 * hh, 64 - 64 * hh
                    dve.wait_ge(s_qk, 4 * (KD + a) + hh + 1)
                    nc.vector.tensor_tensor(q_st[other:other + 64, 2 * a + hh, :], f[me:me + 64],
                                            q_st[me:me + 64, 2 * a + hh, :].bitcast(F32), ALU.subtract
                                            ).then_inc(s_qk, 1)

            def split_k(a):
                f = qk_f[:, a % 2, :]
                for hh in range(2):
                    me = 64 * hh
                    nc.vector.tensor_copy(k_hi[me:me + 64, 2 * a + hh, :], f[me:me + 64]).then_inc(s_qk, 1)
                for hh in range(2):
                    me = 64 * hh
                    dve.wait_ge(s_qk, 4 * a + hh + 1)
                    nc.vector.tensor_tensor(k_lo[me:me + 64, 2 * a + hh, :], f[me:me + 64],
                                            k_hi[me:me + 64, 2 * a + hh, :].bitcast(F32), ALU.subtract
                                            ).then_inc(s_qk, 1)

            dve.wait_ge(s_keys, EDGE_KEYS)
            dve.wait_ge(s_fill, 9)
            one_hots(0)
            factors0()
            one_hots(1)
            masks()
            for w in range(NW):
                if w + 2 < NW:
                    one_hots(w + 2)
                if w == 2:
                    biases()
                residual(w)
                for u in side[w]:
                    unit_part(u)

            for u in schedule:
                if u[0] == "ln":
                    it = u[1]
                    dve.wait_ge(s_acc, it + 1)
                    chain(nc.vector.tensor_tensor(self_sum[:, it, :], banks[:, it, :], self_sum[:, it, :],
                                                  ALU.add))
                    chain(nc.vector.scalar_tensor_tensor(out=xs[:, it, :], in0=self_sum[:, it, :], scalar=0.0,
                                                         in1=xs[:, it, :], op0=ALU.max, op1=ALU.add))
                    statistics(1, it).then_inc(s_var, 1)
                    dve.wait_ge(s_std, 2 + it)
                    chain(nc.vector.reciprocal(rstd[:, 1, it, 1:2], rstd[:, 1, it, 0:1]))
                    if it >= 2:
                        dve.wait_ge(s_unit, number[("h2T", it - 2, 0)] + 1)
                    normalise(1, it, ybuf[:, it % 2, :])
                elif u[0] != "gemm":
                    unit_part(u)

            for step in attention:
                kind, n = step
                if kind == "smax":
                    it, h = divmod(n, H)
                    dve.wait_ge(s_sc, n + 1)
                    dve.wait_ge(s_mask, 2 * (it + 1))
                    if n >= NS:
                        dve.wait_ge(s_exp, n - NS + 1)
                    c = 2 * (n % 2)
                    nc.vector.tensor_tensor_reduce(
                        s_sb[:, n % NS, :].rearrange("p (a j) -> p a j", a=2), banks[:, c:c + 2, 0:HALF],
                        mask_add[:, it, :].rearrange("p (a j) -> p a j", a=2), 1.0, 3.0e38, ALU.add, ALU.min,
                        neg_max[:, it, h:h + 1]).then_inc(s_smax, 1)
                elif kind == "fill" and n % 2 == 1:
                    dve.wait_ge(s_tr, n + 1)
                    if 4 * n + 3 >= NT * H:
                        dve.wait_ge(s_pv, (4 * n + 3 - NT * H) // (2 * NT) + 1)
                    nc.vector.tensor_copy(pT[:, 4 * n % (NT * H):4 * n % (NT * H) + 4, :],
                                          banks[:, 5 + n % 2, :].rearrange("p (s i) -> p s i", s=4)
                                          ).then_inc(s_ptd, 1)
                elif kind == "norm":
                    dve.wait_ge(s_exp, H * (n + 1))
                    if n >= 2:
                        dve.wait_ge(s_rb, n - 1)
                    chain(nc.vector.reciprocal(recip[:, n % 2, :], denom[:, n, :]))
                    nc.vector.scalar_tensor_tensor(out=norm[:, n % 2, :], in0=neg_max[:, n, :], scalar=BIG / 2,
                                                   in1=recip[:, n % 2, :], op0=ALU.is_lt, op1=ALU.mult
                                                   ).then_inc(s_norm, 1)
                elif kind == "msg":
                    dve.wait_ge(s_pv, KD * (n + 1))
                    dve.wait_ge(s_rsb, n + 1)
                    if n >= 1:
                        dve.wait_ge(s_mlo, n)
                    nc.vector.tensor_tensor(msg_f[:], banks[:, 4, :].rearrange("p (a i) -> p a i", a=KD), r_sb[:],
                                            ALU.mult).then_inc(s_msg, 1)
                elif kind == "out":
                    dve.wait_ge(s_ff, n + 1)
                    dve.wait_ge(s_xb, n + 1)
                    if n >= 2:
                        dve.wait_ge(s_out[n % 2], 16 * (n // 2))
                    nc.vector.tensor_tensor(ybuf[:, n % 2, :], banks[:, 7, :], xs[:, n, :], ALU.add
                                            ).then_inc(s_fin, 1)

        @block.tensor
        def _(pe):
            mm = nc.tensor.matmul
            PASSES = ((0, 0), (0, 1), (1, 0))

            pe.wait_ge(s_fill, 4)
            pe.wait_ge(s_keys, 2)
            for k in range(2):
                ins = mm(banks[0:NW, 2, k * EC:(k + 1) * EC], chunk_mm[:, k:k + 1].broadcast_to([EC, NW]),
                         ident[0:EC, 0:EC], start=(k == 0), stop=True, skip_group_check=True)
            ins.then_inc(s_prep, 1)
            pe.wait_ge(s_keys, WINDOW_CHUNKS)
            for k, col in enumerate((2, 1)):
                ins = mm(banks[0:1, 3, k * NW:(k + 1) * NW], win_c[:, col:col + 1], ident[0:NW, 0:NW],
                         start=(k == 0), stop=True, skip_group_check=True)
            ins.then_inc(s_prep, 1)
            for k in range(2):
                nc.tensor.transpose(banks[0:EL, 4, k * EC:(k + 1) * EC], edges_f[:, k, :], ident[0:EC, 0:EC])
            nc.tensor.transpose(banks[:, 4, 160:160 + NT], ntype_f[:], ident[0:NT, 0:NT]).then_inc(s_prep, 1)

            pe.wait_ge(s_keys, BOUNDS)
            pe.wait_ge(s_fill, 16)
            lo = load_bounds(pe, nc, bounds, 0, NW, EC)
            hi = load_bounds(pe, nc, bounds, 1, NW, EC)
            widest = pe.value_load(bounds[0:1, 2, 0:1], min_val=1, max_val=EC)
            filled = [pe.alloc_register(name=f"filled_pe_{i}") for i in range(2)]
            for par in range(2):
                pe.sem_inc(s_slot[par], G)
                pe.reg_mov(filled[par], G // 2)

            def turn(w, first):
                par = w % 2
                for k in range(G):
                    if k % (G // 2) == 0:
                        count = pe.snap(filled[par], min_val=1, max_val=1 << 20)
                        pe.wait_ge(s_src[par], count)
                        pe.wait_ge(s_dst[par], count)
                        pe.reg_add(filled[par], filled[par], G // 2)
                    for jt in range(NT):
                        ins = mm(banks[:, w % 2, jt * R * WIN:(jt + 1) * R * WIN],
                                 src_hot[:, par, k, jt * P:(jt + 1) * P], dst_hot[:, par, k, :],
                                 start=(first and k == 0 and jt == 0), stop=True, skip_group_check=True)
                    ins.then_inc(s_slot[par], 1)

            def window(w):
                if w >= 2:
                    pe.wait_ge(s_res, w - 1)
                turn(w, True)
                with pe.If(hi[w] > lo[w] + G):
                    with pe.Fori(lo[w] + G, hi[w], G):
                        turn(w, False)
                mm(banks[:, w % 2, 500:501], ident16[:], ident16[:, 0:1], start=False, stop=True,
                   skip_group_check=True).then_inc(s_win, 1)

            def take_bank(u):
                if number[u] >= 3:
                    pe.wait_ge(s_ufree, number[u] - 2)

            def unit(u):
                kind = u[0]
                take_bank(u)
                b = bank(u)
                if kind in ("hT", "h2T"):
                    it = u[1]
                    if kind == "hT":
                        pe.wait_ge(s_y0, it + 1)
                        rows = in0[:, it, :]
                    else:
                        pe.wait_ge(s_y, it + 1)
                        rows = ybuf[:, it % 2, :]
                    for kt in range(KD):
                        ins = nc.tensor.transpose(b[:, kt * P:(kt + 1) * P], rows[:, kt * P:(kt + 1) * P], ident[:])
                elif kind == "self":
                    _, t, it = u
                    if it == 0:
                        pe.wait_ge(s_wlo, KD * (t + 1))
                    if t == 0:
                        pe.wait_ge(s_ufree, number[("hT", it, 0)] + 1)
                    ins = gemm(b, hT, it, w_hl[t % 2], 0, D)
                elif kind == "cnt":
                    half = u[1]
                    cols = slice(half * HALF, (half + 1) * HALF)
                    if half == 0:
                        pe.wait_ge(s_adj, NW)
                        pe.wait_ge(s_res, NW)
                        pe.wait_ge(s_keys, MASKS)
                        pe.wait_ge(s_fill, 16)
                    for it in range(NT):
                        a, z = max(it * P, half * HALF), min((it + 1) * P, (half + 1) * HALF)
                        if a < z:
                            mm(b[0:R + T, a - half * HALF:z - half * HALF], mask6[:, it, :],
                               ident16[:, a - it * P:z - it * P], start=(a == half * HALF), stop=False,
                               skip_group_check=True)
                    with pe.If(widest > EXACT16 // EL):
                        for r in range(R):
                            for jt in range(NT):
                                mm(b[0:R + T, 0:HALF], sel6[:, r, :], adjT_res[:, jt, r, cols], start=False,
                                   stop=False, skip_group_check=True)
                    for r in range(R):
                        for jt in range(NT):
                            ins = mm(b[0:R + T, 0:HALF], sel6[:, r, :], adjT[:, jt, r, cols], start=False,
                                     stop=(r == R - 1 and jt == NT - 1), skip_group_check=True)
                elif kind == "z":
                    _, r, dt, half = u
                    cols = slice(half * HALF, (half + 1) * HALF)
                    if (r, dt, half) == (0, 0, 0):
                        pe.wait_ge(s_h16lo, NT)
                    feats = slice(dt * P, (dt + 1) * P)
                    pairs = [(p, jt) for jt in range(NT) for p in range(2)]

                    def add(adj, pick, start, stop):
                        for n, (p, jt) in enumerate(pick):
                            ins = mm(b[:, 0:HALF], h16[:, p, jt, feats], adj[:, jt, r, cols],
                                     start=(start and n == 0), stop=(stop and n == len(pick) - 1),
                                     skip_group_check=True)
                        return ins
                    add(adjT, pairs[:-1], True, False)
                    with pe.If(widest > EXACT16 // EL):
                        add(adjT_res, pairs, False, False)
                    ins = add(adjT, pairs[-1:], False, True)
                elif kind == "m":
                    _, it, part = u
                    tiles = range(4) if part == 0 else range(4, NT)
                    items = [(r, jt) for jt in tiles for r in range(R)]

                    def add(adj, pick, start, stop):
                        for n, (r, jt) in enumerate(pick):
                            rows = (jt - tiles[0]) * P
                            ins = mm(b[:, rows:rows + P], adj[:, jt, r, it * P:(it + 1) * P], ident16[:],
                                     start=(start and n == 0), stop=(stop and n == len(pick) - 1),
                                     skip_group_check=True)
                        return ins
                    add(adjT, items[:-1], True, False)
                    with pe.If(widest > EXACT16 // EL):
                        add(adjT_res, items, False, False)
                    ins = add(adjT, items[-1:], False, True)
                elif kind == "wt":
                    _, g, kt = u
                    q = NWT + g
                    pe.wait_ge(s_raw[q % 2], 16 * (q // 2 + 1))
                    for o in range(4):
                        ins = nc.tensor.transpose(b[:, o * P:(o + 1) * P], raw[q % 2][:, o, kt * P:(kt + 1) * P],
                                                  ident[:])
                elif kind in ("q", "k"):
                    _, a, half = u
                    o = (0 if kind == "q" else D) + a * P
                    if u == ("k", 0, 0):
                        pe.wait_ge(s_ufree, number[("h2T", NT - 1, 0)] + 1)
                    n = 0
                    for kt in range(KD):
                        for pw, ph in PASSES:
                            ins = mm(b[:, 0:HALF], wqkvT[:, pw, kt, o:o + P],
                                     h2T[:, ph, kt, half * HALF:(half + 1) * HALF],
                                     start=(n == 0), stop=(n == 3 * KD - 1))
                            n += 1
                else:
                    pe.wait_ge(s_ufree, number[("h2T", u[1], 0)] + 1)
                    ins = gemm(b, h2T, u[1], wqkvT, 2 * D, D)
                ins.then_inc(s_unit, 1)

            def gemm(to, lhs, it, weights, c0, cn, start=True):
                n = 0
                for kt in range(KD):
                    for pl, pw in PASSES:
                        ins = mm(to, lhs[:, pl, kt, it * P:(it + 1) * P], weights[:, pw, kt, c0:c0 + cn],
                                 start=(start and n == 0), stop=(n == 3 * KD - 1), skip_group_check=True)
                        n += 1
                return ins

            for w in range(NW):
                window(w)
                for u in side[w]:
                    unit(u)
                if w == 1:
                    pe.wait_ge(s_bias, 80)
                    nc.tensor.transpose(banks[:, 2, 176:176 + 3 * KD], bqkv_r[:], ident[0:3 * KD, 0:3 * KD]
                                        ).then_inc(s_prep, 1)

            for u in schedule:
                if u[0] == "ln":
                    continue
                if u[0] != "gemm":
                    unit(u)
                    continue
                _, r, it = u
                if it == 0:
                    pe.wait_ge(s_wlo, KD * (T + r + 1))
                    pe.wait_ge(s_ufree, number[("z", r, KD - 1, 1)] + 1)
                if r == 0:
                    mm(banks[:, it, :], cnt6[:, it * P:(it + 1) * P], b0[:], start=True, stop=False,
                       skip_group_check=True)
                ins = gemm(banks[:, it, :], zT[r % 2], it, w_hl[(T + r) % 2], 0, D, start=False)
                if r == R - 1:
                    ins.then_inc(s_acc, 1)
                elif it == NT - 1:
                    ins.then_inc(s_gemm, 1)

            for step in attention:
                kind, n = step
                if kind == "score":
                    it, h = divmod(n, H)
                    if n < H and n % 2 == 0:
                        pe.wait_ge(s_qk, 4 * KD + 4 * (n // 2 + 1))
                    if n == 0:
                        pe.wait_ge(s_kcp, 2 * KD)
                        pe.wait_ge(s_kcl, 2 * KD)
                    if n >= 2:
                        pe.wait_ge(s_smax, n - 1)
                    for half in range(2):
                        cols = slice(half * HALF, (half + 1) * HALF)
                        for p, k in enumerate((k_hi, k_lo)):
                            ins = mm(banks[:, 2 * (n % 2) + half, 0:HALF], q_st[:, h, it * P:(it + 1) * P],
                                     k[:, h, cols], start=(p == 0), stop=(p == 1))
                    ins.then_inc(s_sc, 1)
                elif kind == "turn":
                    pe.wait_ge(s_exp, n + 1)
                    if n == 0:
                        pe.wait_ge(s_ufree, len(ring))
                    for jt in range(NT):
                        s = n * NT + jt
                        f = s // 4
                        if s % 4 == 0 and f >= 2:
                            pe.wait_ge(s_pta if f % 2 == 0 else s_ptd, f // 2)
                        ins = nc.tensor.transpose(banks[:, 5 + f % 2, (s % 4) * P:(s % 4 + 1) * P],
                                                  p_sb[:, n % NPR, jt * P:(jt + 1) * P], ident[:])
                        if s % 4 == 3:
                            ins.then_inc(s_tr, 1)
                elif kind == "pv":
                    it, a = divmod(n, KD)
                    f = ((2 * n + 2) * NT - 1) // 4
                    pe.wait_ge(s_pta, (f + 2) // 2)
                    pe.wait_ge(s_ptd, (f + 1) // 2)
                    if a == 0 and it >= 1:
                        pe.wait_ge(s_msg, it)
                    for jt in range(NT):
                        for hh in range(2):
                            s = ((2 * n + hh) * NT + jt) % (NT * H)
                            h = 2 * a + hh
                            ins = mm(banks[64 * hh:64 * hh + 64, 4, a * P:(a + 1) * P],
                                     v_sb[:, jt, h * DK:(h + 1) * DK], pT[:, s, :],
                                     start=(jt == 0), stop=(jt == NT - 1), skip_group_check=True)
                    ins.then_inc(s_pv, 1)
                elif kind == "rb":
                    pe.wait_ge(s_norm, n + 1)
                    if n >= 1:
                        pe.wait_ge(s_fin, n)
                    for h in range(H):
                        me = 64 * (h % 2)
                        ins = mm(banks[me:me + 64, 7, h // 2 * P:(h // 2 + 1) * P],
                                 norm[:, n % 2, h:h + 1].broadcast_to([P, DK]), ident[:],
                                 start=(h < 2), stop=True, skip_group_check=True)
                    ins.then_inc(s_rb, 1)
                elif kind == "ff":
                    pe.wait_ge(s_mlo, n + 1)
                    pe.wait_ge(s_rsb, n + 1)
                    k = 0
                    for kt in range(KD):
                        for pl, pw in PASSES:
                            ins = mm(banks[:, 7, :], msgT[:, n % 2, pl, kt, :], wffT[:, pw, kt, :],
                                     start=(k == 0), stop=(k == 3 * KD - 1))
                            k += 1
                    ins.then_inc(s_ff, 1)


def load_bounds(eng, nc, bounds, row, nw, last):
    _, values = nc.values_load_multi_w_load_instructions(
        bounds[0:1, row, 0:nw], engines=(eng.engine,), min_val=0, max_val=last,
        skip_runtime_bounds_check_because="the vector engine clamped them")
    return values


INPUTS = ["x", "src", "dst", "edge_type_3", "node_type_3", "L0_gnn_W_rel", "L0_gnn_b_rel", "L0_gnn_W_self",
          "L0_gnn_b_self", "L1_gnn_W_qkv", "L1_gnn_b_qkv", "L1_gnn_W_ff", "L1_gnn_b_ff"]


def kernel(**inputs):
    import numpy as np
    import concourse.bacc as bacc
    from concourse.bass_utils import run_bass_kernel_spmd

    nc = bacc.Bacc("TRN2", target_bir_lowering=False, num_devices=1)
    arrays, args = {}, []
    for name in INPUTS:
        a = np.ascontiguousarray(inputs[name])
        arrays[f"in_{name}_dram"] = a
        args.append(nc.dram_tensor(f"in_{name}_dram", a.shape, mybir.dt.from_np(a.dtype), kind="ExternalInput").ap())
    shape = inputs["x"].shape
    args.append(nc.dram_tensor("out_0_dram", shape, F32, kind="ExternalOutput").ap())
    gnn_kernel(nc, *args)
    result = run_bass_kernel_spmd(nc, [arrays], core_ids=[0])
    return result.results[0]["out_0_dram"]
```

```python
from contextlib import ExitStack

import concourse.bass as bass
from concourse import mybir

F32 = mybir.dt.float32
F32R = mybir.dt.float32r
F16 = mybir.dt.float16
F8 = mybir.dt.float8e4
I32 = mybir.dt.int32
ALU = mybir.AluOpType
ACT = mybir.ActivationFunctionType
AX = mybir.AxisListType

P = 128
BIG = 1.0e30
EPS = 1e-5
EXACT16 = 2048


def gnn_kernel(nc, x_d, src_d, dst_d, etype_d, ntype_d, wrel_d, brel_d, wself_d, bself_d,
               wqkv_d, bqkv_d, wff_d, bff_d, out_d):
    N, D = x_d.shape
    E = src_d.shape[0]
    R = wrel_d.shape[0]
    T = wself_d.shape[0]
    DK = 64
    H = D // DK
    KD = D // P
    NT = -(-N // P)
    NP = NT * P
    LAST = N - (NT - 1) * P
    EL = 125
    EC = E // EL
    WIN = 32
    NW = NP // WIN
    G = 6
    HALF = NP // 2
    NWT = R + T
    SCALE = float(DK) ** -0.5
    BG = 32
    BROWS = 2 * BG + R + T
    NS, NPR = 3, 6
    assert (N, D, E, R, T) == (625, 512, 10000, 3, 3) and EC * EL == E

    with ExitStack() as ctx:
        def sb(name, shape, dt):
            return ctx.enter_context(nc.sbuf_tensor(name, shape, dt))

        def sem(name):
            return ctx.enter_context(nc.semaphore(name))

        xs = sb("xs", [P, NT, D], F32)
        ident = sb("ident", [P, P], F32)
        ident16 = sb("ident16", [P, P], F16)
        bhl = sb("bhl", [BROWS, D], F32R)
        bv_rows = sb("bv_rows", [P, D], F32)
        bff_rows = sb("bff_rows", [P, D], F32)
        ybuf = sb("ybuf", [P, 2, D], F32)
        edges_i = sb("edges_i", [EC, 3, EL], I32)
        edge_keys = sb("edge_keys", [P, 2, 96], F32)
        ntype_i = sb("ntype_i", [NT, P], I32)
        ntype_f = sb("ntype_f", [NT, P], F32)
        type_mask = sb("type_mask", [P, NT, T], F32)
        mask6 = sb("mask6", [P, NT, BROWS], F16)
        sel6 = sb("sel6", [P, R, BROWS], F16)
        cnt6 = sb("cnt6", [BROWS, NP], F32R)
        bqkv_r = sb("bqkv_r", [3 * KD, P], F32)
        bqk = sb("bqk", [P, 2 * KD], F32)
        chunk_mm = sb("chunk_mm", [EC, 2], F32)
        win_iota = sb("win_iota", [NW, 2], F32)
        c_iota = sb("c_iota", [NW, 2, EC], F32)
        cover = ybuf[0:NW, 1, 0:3 * EC].rearrange("w (k c) -> w k c", k=3)
        win_c = sb("win_c", [NW, 4], F32)
        bounds = sb("bounds", [1, 3, 32], I32)
        bounds_f = sb("bounds_f", [1, 4, 32], F32)
        stats = sb("stats", [P, NT, 6], F32)
        mv = sb("mv", [P, 2, NT, 2], F32)
        rstd = sb("rstd", [P, 2, NT, 2], F32)
        warm = sb("warm", [P, 2], F32)
        shift = sb("shift", [P, 2, NT], F32)
        eps_c = sb("eps_c", [P, 1], F32)
        mask_add = sb("mask_add", [P, NT, NP], F32)
        neg_max = sb("neg_max", [P, NT, H], F32)
        denom = sb("denom", [P, NT, H], F32)
        recip = sb("recip", [P, 2, H], F32)
        norm = sb("norm", [P, 2, H], F32)

        Z_BYTES = 2 * KD * NP * 4
        W_BYTES = 2 * KD * D * 4
        RAW_BYTES = KD * D * 4
        ctx.enter_context(nc.sbuf_tensor("arena", [P, 167936 // 4], F32))
        arena0 = nc.sbuf_base - 167936

        def place(name, offset, shape, dt):
            return nc.alloc_sbuf_tensor_at(name, shape, dt, offset=arena0 + offset)

        o_z1, o_z0 = 0, Z_BYTES
        o_w = 2 * Z_BYTES
        o_raw = o_w + 2 * W_BYTES
        o_r4 = o_raw + 2 * RAW_BYTES + 2048
        o_ss = o_r4 + 4 * 4 * D * 2 * 4
        hT = place("hT", o_z1, [P, 2, KD, NP], F32R)
        zT = [place("zT_even", o_z0, [P, 2, KD, NP], F32R), place("zT_odd", o_z1, [P, 2, KD, NP], F32R)]
        h2T = place("h2T", o_z1, [P, 2, KD, NP], F32R)
        w_hl = [place(f"w_hl{i}", o_w + i * W_BYTES, [P, 2, KD, D], F32R) for i in range(2)]
        raw = [place(f"raw{i}", o_raw + i * RAW_BYTES, [P, KD, D], F32) for i in range(2)]
        h16 = place("h16", o_r4, [P, 2, NT, D], F16)
        adjT = place("adjT", o_r4 + 10240, [P, NT, R, NP], F16)
        adjT_res = place("adjT_res", o_r4 + 29440, [P, NT, R, NP], F8)
        src_hot = place("src_hot", o_r4 + 39040, [P, 2, G, NP], F16)
        dst_hot = place("dst_hot", o_r4 + 54400, [P, 2, G, R * WIN], F16)
        iota = place("iota", o_r4 + 56704, [P, R, NP], F16)
        mcount = place("mcount", o_r4 + 39040, [P, 2, 512], F32)
        edges_f = place("edges_f", o_r4 + 60544, [EC, 2, EL], F32)
        mlog = place("mlog", o_r4 + 43136, [P, 2, 512], F32)
        self_sum = place("self_sum", o_ss, [P, NT, D], F32)
        in0 = place("in0", o_z0, [P, NT, D], F32)
        wqkvT = place("wqkvT", o_r4, [P, 2, KD, 3 * D], F32R)
        wffT = place("wffT", o_r4 + 49152, [P, 2, KD, D], F32R)
        q_st = place("q_st", o_z0, [P, H, NP], F32R)
        k_hi = place("k_hi", o_z0 + 20480, [P, H, NP], F32R)
        k_lo = place("k_lo", o_z0 + 40960, [P, H, NP], F32R)
        v_sb = place("v_sb", o_z0 + 61440, [P, NT, D], F32)
        qk_f = place("qk_f", o_ss, [P, 2, NP], F32)
        s_sb = place("s_sb", o_r4, [P, NS, NP], F32)
        p_sb = place("p_sb", o_r4 + 7680, [P, NPR, NP], F32)
        pT = place("pT", o_z1, [P, NT * H, P], F32)
        msg_f = place("msg_f", o_r4 + 23040, [P, KD, P], F32)
        r_sb = place("r_sb", o_r4 + 25088, [P, KD, P], F32)
        msgT = place("msgT", o_r4 + 27136, [P, 2, 2, KD, P], F32R)

        banks = ctx.enter_context(nc.psum_tensor("banks", [P, 8, 512], F32))

        s_fill = sem("s_fill")
        s_edges = sem("s_edges")
        s_nodes = sem("s_nodes")
        s_x = sem("s_x")
        s_bias = sem("s_bias")
        s_b0 = sem("s_b0")
        s_bhi = sem("s_bhi")
        s_blo = sem("s_blo")
        s_raw = [sem("s_raw0"), sem("s_raw1")]
        s_keys = sem("s_keys")
        s_prep = sem("s_prep")
        s_chain = sem("s_chain")
        s_src = [sem("s_src0"), sem("s_src1")]
        s_dst = [sem("s_dst0"), sem("s_dst1")]
        s_slot = [sem("s_slot0"), sem("s_slot1")]
        s_win = sem("s_win")
        s_adj = sem("s_adj")
        s_res = sem("s_res")
        s_var = sem("s_var")
        s_factor = sem("s_factor")
        s_std = sem("s_std")
        s_y0 = sem("s_y0")
        s_y = sem("s_y")
        s_h16hi = sem("s_h16hi")
        s_whi = sem("s_whi")
        s_wlo = sem("s_wlo")
        s_unit = sem("s_unit")
        s_uhi = sem("s_uhi")
        s_ufree = sem("s_ufree")
        s_gemm = sem("s_gemm")
        s_acc = sem("s_acc")
        s_mc = sem("s_mc")
        s_ln = sem("s_ln")
        s_h16lo = sem("s_h16lo")
        s_mask = sem("s_mask")
        s_qk = sem("s_qk")
        s_qhi = sem("s_qhi")
        s_kcp = sem("s_kcp")
        s_kcl = sem("s_kcl")
        s_kcd = sem("s_kcd")
        s_sc = sem("s_sc")
        s_smax = sem("s_smax")
        s_exp = sem("s_exp")
        s_tr = sem("s_tr")
        s_pta = sem("s_pta")
        s_ptd = sem("s_ptd")
        s_pv = sem("s_pv")
        s_norm = sem("s_norm")
        s_rb = sem("s_rb")
        s_rsb = sem("s_rsb")
        s_msg = sem("s_msg")
        s_mhi = sem("s_mhi")
        s_mlo = sem("s_mlo")
        s_ff = sem("s_ff")
        s_xb = sem("s_xb")
        s_fin = sem("s_fin")
        s_out = [sem("s_out0"), sem("s_out1")]

        side = {w: [] for w in range(NW)}
        side[0] = [("hT", 0, 0), ("hT", 1, 0)]
        for it in range(2, NT):
            side[it - 1].append(("hT", it, 0))
        for n in range(T * NT):
            side[1 + n].append(("self", n // NT, n % NT))
        first_half = [("cnt", 0, 0)] + [("z", 0, dt, 0) for dt in range(KD)]
        for n, u in enumerate(first_half):
            side[NW - len(first_half) + n].append(u)

        def z_units(r):
            return [("z", r, dt, half) for dt in range(KD) for half in range(2)]

        schedule = [u for u in [("cnt", 1, 0)] + z_units(0) + z_units(1) if u not in first_half]
        for it in range(NT):
            schedule += [("gemm", 0, it), ("m", it, 0), ("m", it, 1)]
        schedule += z_units(2)
        wt_units = [("wt", g, kt) for g in range(3) for kt in range(KD)]
        for it in range(NT):
            schedule += [("gemm", 1, it)] + wt_units[3 * it:3 * it + 3]
        schedule += [("wt", 3, 0), ("wt", 3, 1)]
        for it in range(NT):
            schedule += [("gemm", 2, it), ("sum", it)]
            if it >= 2:
                schedule.append(("h2T", it - 2, 0))
            schedule.append(("ln", it))
            if it == 0:
                schedule += [("wt", 3, 2), ("wt", 3, 3)]
        schedule += [("v", 0, 0), ("v", 1, 0), ("h2T", 3, 0), ("v", 2, 0), ("h2T", 4, 0), ("v", 3, 0), ("v", 4, 0)]
        schedule += [("k", a, half) for a in range(KD) for half in range(2)]
        schedule += [("q", a, half) for a in range(KD) for half in range(2)]
        ring = [u for w in range(NW) for u in side[w]] + [u for u in schedule if u[0] not in ("gemm", "sum", "ln")]
        number = {u: n for n, u in enumerate(ring)}

        def bank(u):
            return banks[:, 5 + number[u] % 3, :]

        def used_weights(eng, q):
            if q < T:
                eng.wait_ge(s_unit, number[("self", q, NT - 1)] + 1)
            else:
                eng.wait_ge(s_gemm, q - T + 1)

        act_units = [u for u in ring if u[0] in ("hT", "z", "wt", "h2T", "q", "k")]
        act_done = {u: n + 1 for n, u in enumerate(act_units)}
        m_units = [u for u in ring if u[0] == "m"]

        def m_cols(part):
            return (0, 4 * P) if part == 0 else (4 * P, P)

        TURN, PV, RB, FF, FF_STEP = 3.2, 2.8, 10.8, 2.2, 0.3
        placed = []
        for n in range(NT * H):
            placed += [(n, "score", n), (n + 0.1, "smax", n), (n + 0.7, "exp", n)]
        turn_at = [TURN + 4 * f / NT for f in range(NT * NT * H // 4)]
        for f, at in enumerate(turn_at):
            placed += [(at, "turn", f), (at + 0.1, "fill", f)]
        pv_at = [turn_at[((2 * n + 2) * NT - 1) // 4] + PV for n in range(NT * KD)]
        placed += [(at, "pv", n) for n, at in enumerate(pv_at)]
        for it in range(NT):
            msg_at = max(pv_at[(it + 1) * KD - 1], it * H + RB) + 0.1
            placed += [((it + 1) * H, "norm", it), (it * H + RB, "rb", it)]
            placed += [(msg_at, "msg", it * KD + a) for a in range(KD)]
            placed += [(msg_at + FF + FF_STEP * kt, "ff", it * KD + kt) for kt in range(KD)]
            placed.append((msg_at + FF + FF_STEP * (KD - 1) + 0.1, "out", it))
        attention = [(kind, n) for _, kind, n in sorted(placed, key=lambda step: step[0])]

        KCOPY = [(a, hh) for a in range(KD) for hh in range(2)]
        KCOPY_DVE = [(a, 1) for a in range(KD - 2, KD)]
        KCOPY_POOL = [c for c in KCOPY if c not in KCOPY_DVE]

        def split_count(n):
            return 4 * min(n, KD) + 2 * max(n - KD, 0)

        WINDOW_CHUNKS, BOUNDS, EDGE_KEYS, MASKS, BIASES = 6, 9, 10, 16, 18

        BIASES_IN = 9 * 16
        b_raw = ybuf[0:BROWS, 0, :]

        block = ctx.enter_context(nc.Block())

        @block.sync
        def _(sp):
            for k, arr in ((1, dst_d), (2, etype_d), (0, src_d)):
                sp.dma_start(edges_i[:, k, :], arr.rearrange("(c p) -> c p", p=EL)).then_inc(s_edges, 16)
            sp.wait_ge(s_fill, 2)
            sp.dma_start(xs[:, 0:NT - 1, :], x_d[0:(NT - 1) * P, :].rearrange("(t p) d -> p t d", p=P)
                         ).then_inc(s_x, 16)
            sp.dma_start(xs[0:LAST, NT - 1, :], x_d[(NT - 1) * P:N, :]).then_inc(s_x, 16)
            for q in range(NWT + 4):
                if q >= 2 and q - 2 < NWT:
                    sp.wait_ge(s_wlo, KD * (q - 1))
                elif q >= 2:
                    sp.wait_ge(s_unit, number[("wt", q - 2 - NWT, KD - 1)] + 1)
                if q < T:
                    w = wself_d[q].rearrange("(k p) n -> p k n", p=P)
                elif q < NWT:
                    w = wrel_d[q - T].rearrange("(k p) n -> p k n", p=P)
                elif q < NWT + 3:
                    w = wqkv_d[(q - NWT) * D:(q - NWT + 1) * D, :].rearrange("(k p) n -> p k n", p=P)
                else:
                    w = wff_d.rearrange("(k p) n -> p k n", p=P)
                sp.dma_start(raw[q % 2][:], w).then_inc(s_raw[q % 2], 16)
            for it in range(NT):
                rows = P if it < NT - 1 else LAST
                sp.wait_ge(s_fin, it + 1)
                sp.dma_start(out_d[it * P:it * P + rows, :], ybuf[0:rows, it % 2, :]).then_inc(s_out[it % 2], 16)
            sp.wait_ge(s_out[0], 16 * -(-NT // 2))
            sp.wait_ge(s_out[1], 16 * (NT // 2))

        @block.gpsimd
        def _(pool):
            nc.gpsimd.memset(ntype_i[:], 0).then_inc(s_fill, 1)
            nc.gpsimd.memset(xs[:, NT - 1, :], 0.0).then_inc(s_fill, 1)
            nc.gpsimd.memset(ident[:], 0.0).then_inc(s_fill, 1)
            pool.wait_ge(s_fill, 3)
            nc.gpsimd.affine_select(out=ident[:], in_=ident[:], compare_op=ALU.not_equal, fill=1.0, base=0,
                                    pattern=[[-1, P]], channel_multiplier=1).then_inc(s_fill, 1)
            nc.gpsimd.iota(win_iota[:], [[WIN, 2]], base=0, channel_multiplier=WIN,
                           allow_small_or_imprecise_dtypes=True).then_inc(s_fill, 1)
            nc.gpsimd.iota(c_iota[:, 0, :], [[1, EC]], base=1, channel_multiplier=0,
                           allow_small_or_imprecise_dtypes=True).then_inc(s_fill, 1)
            nc.gpsimd.iota(c_iota[:, 1, :], [[-1, EC]], base=EC, channel_multiplier=0,
                           allow_small_or_imprecise_dtypes=True).then_inc(s_fill, 1)
            nc.gpsimd.memset(edge_keys[:], -1.0).then_inc(s_fill, 1)
            nc.gpsimd.iota(iota[:], [[1, R * NP]], base=0, channel_multiplier=0,
                           allow_small_or_imprecise_dtypes=True).then_inc(s_fill, 1)
            pool.wait_ge(s_fill, 4)
            nc.gpsimd.tensor_copy(ident16[:], ident[:]).then_inc(s_fill, 1)
            nc.gpsimd.memset(sel6[:], 0.0).then_inc(s_fill, 1)
            nc.gpsimd.memset(mask6[:], 0.0).then_inc(s_fill, 1)
            nc.gpsimd.memset(eps_c[:], EPS).then_inc(s_fill, 1)
            pool.wait_ge(s_fill, 11)
            for r in range(R):
                nc.gpsimd.memset(sel6[:, r, r:BROWS:BG], 1.0).then_inc(s_fill, 1)

            def weights_lo(q, kt):
                pool.wait_ge(s_whi, q + 1)
                nc.gpsimd.tensor_tensor(w_hl[q % 2][:, 1, kt], raw[q % 2][:, kt],
                                        w_hl[q % 2][:, 0, kt].bitcast(F32), ALU.subtract).then_inc(s_wlo, 1)

            pieces = {0: [(0, 0), (0, 1)], 1: [(0, 2), (0, 3)]}
            for q, w0 in ((1, 2), (2, 6), (3, 11)):
                for kt in range(KD):
                    pieces[w0 + kt] = [(q, kt)]
            for w in range(NW):
                for q, kt in pieces.get(w, []):
                    weights_lo(q, kt)
                if 8 <= w < 8 + NT:
                    it = w - 8
                    pool.wait_ge(s_h16hi, it + 1)
                    nc.gpsimd.tensor_tensor(h16[:, 1, it, :], in0[:, it, :], h16[:, 0, it, :], ALU.subtract
                                            ).then_inc(s_h16lo, 1)
            for kt in range(KD):
                weights_lo(4, kt)
            for n, u in enumerate(m_units):
                _, it, part = u
                c0, cn = m_cols(part)
                pool.wait_ge(s_ln, n + 1)
                pool.wait_ge(s_ufree, number[u] + 1)
                nc.gpsimd.tensor_tensor(mask_add[:, it, c0:c0 + cn], mask_add[:, it, c0:c0 + cn],
                                        mlog[:, n % 2, 0:cn], ALU.subtract).then_inc(s_mask, 1)
            for kt in range(KD):
                weights_lo(5, kt)
            for it in range(NT):
                pool.wait_ge(s_bias, BIASES_IN)
                pool.wait_ge(s_y, it + 1)
                nc.gpsimd.tensor_tensor(xs[:, it, :], xs[:, it, :], bff_rows[:], ALU.add).then_inc(s_xb, 1)
            pool.wait_ge(s_xb, NT)
            for n, (a, hh) in enumerate(KCOPY_POOL):
                pool.wait_ge(s_qk, split_count(a + 1))
                if n:
                    pool.wait_ge(s_kcl, n)
                me, other = 64 * hh, 64 - 64 * hh
                nc.gpsimd.tensor_copy(k_lo[other:other + 64, 2 * a + hh, :],
                                      k_lo[me:me + 64, 2 * a + hh, :].bitcast(F32)).then_inc(s_kcl, 1)
            pool.wait_ge(s_kcl, len(KCOPY_POOL))
            for n in range(NT * KD):
                it, a = divmod(n, KD)
                pool.wait_ge(s_mhi, n + 1)
                nc.gpsimd.tensor_tensor(msgT[:, it % 2, 1, a], msg_f[:, a], msgT[:, it % 2, 0, a].bitcast(F32),
                                        ALU.subtract).then_inc(s_mlo, 1)

        @block.scalar
        def _(act):
            act.wait_ge(s_fill, 1)
            act.dma_start(ntype_i[0:NT - 1, :], ntype_d[0:(NT - 1) * P].rearrange("(t p) -> t p", p=P)
                          ).then_inc(s_nodes, 16)
            act.dma_start(ntype_i[NT - 1:NT, 0:LAST], ntype_d[(NT - 1) * P:N].rearrange("(t p) -> t p", t=1)
                          ).then_inc(s_nodes, 16)
            act.dma_start(bqkv_r[:], bqkv_d.rearrange("(o p) -> o p", p=P)).then_inc(s_bias, 16)
            act.dma_start(bv_rows[:], bqkv_d[2 * D:3 * D].partition_broadcast(P)).then_inc(s_bias, 16)
            act.dma_start(bff_rows[:], bff_d.partition_broadcast(P)).then_inc(s_bias, 16)
            act.wait_ge(s_b0, 1)
            for g in range(3):
                act.dma_start(b_raw[g * BG:g * BG + R, :], brel_d).then_inc(s_bias, 16)
                act.dma_start(b_raw[g * BG + R:g * BG + R + T, :], bself_d).then_inc(s_bias, 16)

            def weights_hi(q):
                act.wait_ge(s_raw[q % 2], 16 * (q // 2 + 1))
                if q >= 2:
                    used_weights(act, q - 2)
                nc.scalar.activation(w_hl[q % 2][:, 0], raw[q % 2][:], ACT.Copy).then_inc(s_whi, 1)

            def standard_deviation(layer, t0, t1, count):
                act.wait_ge(s_var, count)
                nc.scalar.activation(rstd[:, layer, t0:t1, 0], mv[:, layer, t0:t1, 1], ACT.Sqrt,
                                     bias=eps_c[:]).then_inc(s_std, 1)

            def store_window(w):
                act.wait_ge(s_win, w + 1)
                nc.scalar.activation(adjT[:, :, :, w * WIN:(w + 1) * WIN],
                                     banks[:, w % 2, 0:NT * R * WIN].rearrange("p (t r i) -> p t r i", t=NT, r=R),
                                     ACT.Copy).then_inc(s_adj, 1)

            act.wait_ge(s_fill, 16)
            nc.scalar.activation(warm[:, 0:1], eps_c[:], ACT.Sqrt)
            weights_hi(0)
            standard_deviation(0, 0, NT, 1)
            act.wait_ge(s_factor, 1)

            def rows0(it):
                nc.scalar.activation(in0[:, it, :], xs[:, it, :], ACT.Relu, bias=shift[:, 0, it:it + 1],
                                     scale=rstd[:, 0, it, 1:2]).then_inc(s_y0, 1)

            def h16_hi(it):
                act.wait_ge(s_y0, it + 1)
                nc.scalar.activation(h16[:, 0, it, :], in0[:, it, :], ACT.Copy).then_inc(s_h16hi, 1)

            for it in range(NT):
                rows0(it)

            def unit_part(u):
                kind = u[0]
                if kind not in ("hT", "z", "wt", "h2T", "q", "k"):
                    return
                act.wait_ge(s_unit, number[u] + 1)
                if kind == "hT":
                    it = u[1]
                    ins = nc.scalar.activation(hT[:, 0, :, it * P:(it + 1) * P],
                                               bank(u).rearrange("p (k i) -> p k i", k=KD), ACT.Copy)
                elif kind == "h2T":
                    it = u[1]
                    ins = nc.scalar.activation(h2T[:, 0, :, it * P:(it + 1) * P],
                                               bank(u).rearrange("p (k i) -> p k i", k=KD), ACT.Relu)
                elif kind == "z":
                    _, r, dt, half = u
                    if u == ("z", 0, 0, 0):
                        act.wait_ge(s_h16lo, NT)
                    ins = nc.scalar.activation(zT[r % 2][:, 0, dt, half * HALF:(half + 1) * HALF],
                                               bank(u)[:, 0:HALF], ACT.Copy)
                elif kind == "wt":
                    _, g, kt = u
                    if u == ("wt", 0, 0):
                        act.wait_ge(s_mask, len(m_units))
                    to = wqkvT[:, 0, kt, g * D:(g + 1) * D] if g < 3 else wffT[:, 0, kt, :]
                    ins = nc.scalar.activation(to, bank(u), ACT.Copy)
                else:
                    _, a, half = u
                    n = a if kind == "k" else KD + a
                    if n == 0:
                        act.wait_ge(s_keys, BIASES)
                    if n >= 2:
                        act.wait_ge(s_qk, split_count(n - 1))
                    ins = nc.scalar.activation(qk_f[:, n % 2, half * HALF:(half + 1) * HALF], bank(u)[:, 0:HALF],
                                               ACT.Identity, bias=bqk[:, n:n + 1],
                                               scale=-SCALE if kind == "q" else 1.0)
                ins.then_inc(s_uhi, 1)

            w_at = {3: 1, 6: 2, 11: 3, 16: 4}
            for w in range(NW):
                if w >= 1:
                    for u in side[w - 1]:
                        unit_part(u)
                store_window(w)
                if w == 4:
                    act.wait_ge(s_bias, BIASES_IN)
                    nc.scalar.activation(bhl[:], b_raw, ACT.Copy).then_inc(s_bhi, 1)
                if w in w_at:
                    weights_hi(w_at[w])
                if 8 <= w < 8 + NT:
                    h16_hi(w - 8)
            for u in side[NW - 1]:
                unit_part(u)
            n_ln = 0
            for u in schedule:
                if u == ("z", 2, 0, 0):
                    weights_hi(5)
                if u[0] == "m":
                    cn = m_cols(u[2])[1]
                    act.wait_ge(s_mc, n_ln + 1)
                    if n_ln >= 2:
                        act.wait_ge(s_mask, n_ln - 1)
                    nc.scalar.activation(mlog[:, n_ln % 2, 0:cn], mcount[:, n_ln % 2, 0:cn], ACT.Ln
                                         ).then_inc(s_ln, 1)
                    n_ln += 1
                    continue
                if u[0] == "ln":
                    it = u[1]
                    standard_deviation(1, it, it + 1, 2 + it)
                    act.wait_ge(s_factor, 2 + it)
                    if it >= 2:
                        act.wait_ge(s_unit, number[("h2T", it - 2, 0)] + 1)
                    nc.scalar.activation(ybuf[:, it % 2, :], xs[:, it, :], ACT.Identity, bias=shift[:, 1, it:it + 1],
                                         scale=rstd[:, 1, it, 1:2]).then_inc(s_y, 1)
                    if it == NT - 1:
                        nc.scalar.activation(warm[:, 1:2], eps_c[:], ACT.Exp)
                    continue
                if u[0] in ("gemm", "sum"):
                    continue
                unit_part(u)
                if u[0] == "k" and u[2] == 1:
                    a = u[1]
                    for hh in range(2):
                        me, other = 64 * hh, 64 - 64 * hh
                        act.wait_ge(s_qk, 4 * a + hh + 1)
                        nc.scalar.activation(k_hi[other:other + 64, 2 * a + hh, :],
                                             k_hi[me:me + 64, 2 * a + hh, :].bitcast(F32), ACT.Copy
                                             ).then_inc(s_kcp, 1)
                if u[0] == "q" and u[2] == 1:
                    a = u[1]
                    act.wait_ge(s_uhi, act_done[u])
                    for hh in range(2):
                        me = 64 * hh
                        nc.scalar.activation(q_st[me:me + 64, 2 * a + hh, :], qk_f[me:me + 64, (KD + a) % 2, :],
                                             ACT.Copy).then_inc(s_qhi, 1)

            for step in attention:
                kind, n = step
                if kind == "exp":
                    it, h = divmod(n, H)
                    act.wait_ge(s_smax, n + 1)
                    if n >= NPR:
                        act.wait_ge(s_tr, -(-(n - NPR + 1) * NT // 4))
                    nc.scalar.activation(p_sb[:, n % NPR, :], s_sb[:, n % NS, :], ACT.Exp, scale=-1.0,
                                         bias=neg_max[:, it, h:h + 1],
                                         accum_out=denom[:, it, h:h + 1]).then_inc(s_exp, 1)
                elif kind == "fill" and n % 2 == 0:
                    act.wait_ge(s_tr, n + 1)
                    if 4 * n + 3 >= NT * H:
                        act.wait_ge(s_pv, (4 * n + 3 - NT * H) // (2 * NT) + 1)
                    nc.scalar.activation(pT[:, 4 * n % (NT * H):4 * n % (NT * H) + 4, :],
                                         banks[:, 5 + n % 2, :].rearrange("p (s i) -> p s i", s=4), ACT.Copy
                                         ).then_inc(s_pta, 1)
                elif kind == "rb":
                    act.wait_ge(s_rb, n + 1)
                    if n >= 1:
                        act.wait_ge(s_msg, KD * n)
                    nc.scalar.activation(r_sb[:], banks[:, 7, :].rearrange("p (a i) -> p a i", a=KD), ACT.Copy
                                         ).then_inc(s_rsb, 1)
                elif kind == "msg":
                    it, a = divmod(n, KD)
                    act.wait_ge(s_msg, n + 1)
                    if it >= 2:
                        act.wait_ge(s_ff, it - 1)
                    nc.scalar.activation(msgT[:, it % 2, 0, a], msg_f[:, a], ACT.Copy).then_inc(s_mhi, 1)

        @block.vector
        def _(dve):
            links = [0]

            def chain(ins):
                links[0] += 1
                ins.then_inc(s_chain, 1)
                dve.wait_ge(s_chain, links[0])

            nc.vector.memset(b_raw, 0.0).then_inc(s_b0, 1)

            dve.wait_ge(s_edges, 48)
            nc.vector.tensor_reduce(chunk_mm[:, 0:1], edges_i[:, 1, :], AX.X, ALU.min).then_inc(s_keys, 1)
            nc.vector.tensor_reduce(chunk_mm[:, 1:2], edges_i[:, 1, :], AX.X, ALU.max).then_inc(s_keys, 1)
            nc.vector.tensor_copy(edges_f[:, 0, :], edges_i[:, 0, :]).then_inc(s_keys, 1)
            nc.vector.scalar_tensor_tensor(out=edges_f[:, 1, :], in0=edges_i[:, 2, :], scalar=float(NP),
                                           in1=edges_i[:, 1, :], op0=ALU.mult, op1=ALU.add).then_inc(s_keys, 1)
            dve.wait_ge(s_nodes, 32)
            nc.vector.tensor_copy(ntype_f[:], ntype_i[:]).then_inc(s_keys, 1)

            def statistics(layer, it):
                chain(nc.vector.bn_stats(stats[:, it, :], xs[:, it, :]))
                return nc.vector.bn_aggr(mv[:, layer, it, :], stats[:, it, :])

            dve.wait_ge(s_fill, 8)
            dve.wait_ge(s_prep, 1)
            low = banks[0:NW, 2, 0:EC]
            high = banks[0:NW, 2, EC:2 * EC]
            chain(nc.vector.tensor_scalar(cover[:, 0, :], low, win_iota[:, 1:2], None, ALU.is_lt))
            chain(nc.vector.scalar_tensor_tensor(out=cover[:, 1, :], in0=high, scalar=win_iota[:, 0:1],
                                                 in1=cover[:, 0, :], op0=ALU.is_ge, op1=ALU.mult))
            chain(nc.vector.tensor_tensor_reduce(cover[:, 2, :], cover[:, 1, :], c_iota[:, 0, :], 1.0, 0.0,
                                                 ALU.mult, ALU.max, win_c[:, 1:2]))
            chain(nc.vector.tensor_tensor_reduce(cover[:, 2, :], cover[:, 1, :], c_iota[:, 1, :], 1.0, 0.0,
                                                 ALU.mult, ALU.max, win_c[:, 0:1]))
            chain(nc.vector.tensor_scalar(win_c[:, 0:1], win_c[:, 0:1], -1.0, float(EC), ALU.mult, ALU.add))
            nc.vector.tensor_scalar(win_c[:, 2:3], win_c[:, 0:1], float(EC - 1), None, ALU.min
                                    ).then_inc(s_keys, 1)
            dve.wait_ge(s_x, 32)
            statistics(0, 0)
            dve.wait_ge(s_prep, 2)
            brow = banks[0:1, 3, 0:2 * NW]
            chain(nc.vector.tensor_copy(bounds_f[:, 0:2, 0:NW], brow.rearrange("p (b w) -> p b w", b=2)))
            chain(nc.vector.scalar_tensor_tensor(out=bounds_f[:, 2, 0:NW], in0=bounds_f[:, 0, 0:NW], scalar=1.0,
                                                 in1=bounds_f[:, 1, 0:NW], op0=ALU.add, op1=ALU.max))
            chain(nc.vector.tensor_tensor(bounds_f[:, 3, 0:NW], bounds_f[:, 2, 0:NW], bounds_f[:, 0, 0:NW],
                                          ALU.subtract))
            chain(nc.vector.tensor_reduce(bounds_f[:, 3, 31:32], bounds_f[:, 3, 0:NW], AX.X, ALU.max))
            nc.vector.tensor_copy(bounds[:, 0, 0:NW], bounds_f[:, 0, 0:NW]).then_inc(s_keys, 1)
            nc.vector.tensor_copy(bounds[:, 1, 0:NW], bounds_f[:, 2, 0:NW]).then_inc(s_keys, 1)
            nc.vector.tensor_copy(bounds[:, 2, 0:1], bounds_f[:, 3, 31:32]).then_inc(s_keys, 1)
            dve.wait_ge(s_prep, 3)
            nc.vector.tensor_copy(edge_keys[0:EL, :, 0:EC], banks[0:EL, 4, 0:2 * EC].rearrange("p (k c) -> p k c", k=2)
                                  ).then_inc(s_keys, 1)
            for it in range(1, NT):
                ins = nc.vector.bn_stats(stats[:, it, :], xs[:, it, :])
            links[0] += 1
            ins.then_inc(s_chain, 1)
            dve.wait_ge(s_keys, BOUNDS)
            lo = load_bounds(dve, nc, bounds, 0, NW, EC)
            asked = [dve.alloc_register(name=f"asked_dve_{i}") for i in range(2)]
            for par in range(2):
                dve.reg_mov(asked[par], G // 2)

            dve.wait_ge(s_chain, links[0])
            for it in range(1, NT):
                ins = nc.vector.bn_aggr(mv[:, 0, it, :], stats[:, it, :])
            ins.then_inc(s_var, 1)

            def masks():
                for t in range(T):
                    nc.vector.tensor_scalar(type_mask[:, :, t], banks[:, 4, 160:160 + NT], float(t), None,
                                            ALU.is_equal).then_inc(s_keys, 1)
                dve.wait_ge(s_fill, 16)
                dve.wait_ge(s_keys, MASKS - 3)
                for g in range(3):
                    nc.vector.tensor_copy(mask6[:, :, g * BG + R:g * BG + R + T], type_mask[:]
                                          ).then_inc(s_keys, 1)

            def biases():
                dve.wait_ge(s_prep, 4)
                nc.vector.tensor_copy(bqk[:, 0:KD], banks[:, 2, 176 + KD:176 + 2 * KD]).then_inc(s_keys, 1)
                nc.vector.tensor_scalar(bqk[:, KD:2 * KD], banks[:, 2, 176:176 + KD], -SCALE, None, ALU.mult
                                        ).then_inc(s_keys, 1)

            def factors(layer, t0, t1):
                chain(nc.vector.reciprocal(rstd[:, layer, t0:t1, 1], rstd[:, layer, t0:t1, 0]))
                nc.vector.scalar_tensor_tensor(out=shift[:, layer, t0:t1], in0=mv[:, layer, t0:t1, 0], scalar=-1.0,
                                               in1=rstd[:, layer, t0:t1, 1], op0=ALU.mult, op1=ALU.mult
                                               ).then_inc(s_factor, 1)

            def hot_group(w, c, ks=range(G)):
                par = w % 2
                for k in ks:
                    if k % (G // 2) == 0:
                        dve.wait_ge(s_slot[par], dve.snap(asked[par], min_val=1, max_val=1 << 20))
                        dve.reg_add(asked[par], asked[par], G // 2)
                        g, n = slice(k, k + G // 2), G // 2
                        nc.vector.tensor_tensor(
                            dst_hot[:, par, g].rearrange("p g (r i) -> p g r i", r=R),
                            iota[:, :, w * WIN:(w + 1) * WIN].unsqueeze(1).broadcast_to([P, n, R, WIN]),
                            edge_keys[:, 1, bass.ds(c + k, n)].unsqueeze(2).unsqueeze(3)
                            .broadcast_to([P, n, R, WIN]), ALU.is_equal).then_inc(s_dst[par], n)
                    nc.vector.tensor_scalar(src_hot[:, par, k, :], iota[:, 0, :],
                                            edge_keys[:, 0, bass.ds(c + k, 1)], None, ALU.is_equal
                                            ).then_inc(s_src[par], 1)

            def further_groups(w):
                with dve.If(hi[w] > lo[w] + G):
                    with dve.Fori(lo[w] + G, hi[w], G) as c:
                        hot_group(w, c)

            def residual(w):
                dve.wait_ge(s_adj, w + 1)
                with dve.If(widest > EXACT16 // EL):
                    nc.vector.tensor_tensor(
                        adjT_res[:, :, :, w * WIN:(w + 1) * WIN],
                        banks[:, w % 2, 0:NT * R * WIN].rearrange("p (t r i) -> p t r i", t=NT, r=R),
                        adjT[:, :, :, w * WIN:(w + 1) * WIN], ALU.subtract, saturate=False)
                nc.vector.engine_nop().then_inc(s_res, 1)

            def unit_part(u):
                kind = u[0]
                b = bank(u)
                dve.wait_ge(s_unit, number[u] + 1)
                if u in act_done:
                    dve.wait_ge(s_uhi, act_done[u])
                if kind in ("hT", "h2T"):
                    it = u[1]
                    to = hT if kind == "hT" else h2T
                    nc.vector.scalar_tensor_tensor(
                        out=to[:, 1, :, it * P:(it + 1) * P], in0=b.rearrange("p (k i) -> p k i", k=KD), scalar=0.0,
                        in1=to[:, 0, :, it * P:(it + 1) * P].bitcast(F32), op0=ALU.max, op1=ALU.subtract
                    ).then_inc(s_ufree, 1)
                elif kind == "self":
                    _, t, it = u
                    m = type_mask[:, it, t:t + 1]
                    if t == 0:
                        nc.vector.tensor_scalar(self_sum[:, it, :], b, m, None, ALU.mult).then_inc(s_ufree, 1)
                    else:
                        dve.wait_ge(s_ufree, number[("self", t - 1, it)] + 1)
                        nc.vector.scalar_tensor_tensor(out=self_sum[:, it, :], in0=b, scalar=m,
                                                       in1=self_sum[:, it, :], op0=ALU.mult, op1=ALU.add
                                                       ).then_inc(s_ufree, 1)
                elif kind == "cnt":
                    half = u[1]
                    cols = slice(half * HALF, (half + 1) * HALF)
                    lo_rows = slice(2 * BG, BROWS)
                    chain(nc.vector.tensor_copy(cnt6[:, cols], b[0:BROWS, 0:HALF]))
                    nc.vector.tensor_tensor(cnt6[lo_rows, cols], b[lo_rows, 0:HALF],
                                            cnt6[lo_rows, cols].bitcast(F32), ALU.subtract).then_inc(s_ufree, 1)
                elif kind == "z":
                    _, r, dt, half = u
                    cols = slice(half * HALF, (half + 1) * HALF)
                    nc.vector.tensor_tensor(zT[r % 2][:, 1, dt, cols], b[:, 0:HALF],
                                            zT[r % 2][:, 0, dt, cols].bitcast(F32), ALU.subtract
                                            ).then_inc(s_ufree, 1)
                elif kind == "wt":
                    _, g, kt = u
                    to = (lambda part: wqkvT[:, part, kt, g * D:(g + 1) * D]) if g < 3 else \
                         (lambda part: wffT[:, part, kt, :])
                    nc.vector.tensor_tensor(to(1), b, to(0).bitcast(F32), ALU.subtract).then_inc(s_ufree, 1)
                elif kind == "m":
                    _, it, part = u
                    n = m_units.index(u)
                    c0, cn = m_cols(part)
                    if n >= 2:
                        dve.wait_ge(s_ln, n - 1)
                    nc.vector.tensor_scalar(mcount[:, n % 2, 0:cn], b[:, 0:cn], 1.0, None, ALU.max
                                            ).then_inc(s_mc, 1)
                    nc.vector.tensor_scalar(mask_add[:, it, c0:c0 + cn], b[:, 0:cn], 0.0, BIG,
                                            ALU.is_equal, ALU.mult).then_inc(s_ufree, 1)
                elif kind == "v":
                    jt = u[1]
                    dve.wait_ge(s_bias, BIASES_IN)
                    nc.vector.tensor_tensor(v_sb[:, jt, :], b, bv_rows[:], ALU.add).then_inc(s_ufree, 1)
                elif kind == "q":
                    nc.vector.engine_nop().then_inc(s_ufree, 1)
                    if u[2] == 1 and u[1] < KD - 1:
                        split_q(u[1])
                else:
                    nc.vector.engine_nop().then_inc(s_ufree, 1)
                    if u[2] == 1:
                        split_k(u[1])

            def split_q(a):
                f = qk_f[:, (KD + a) % 2, :]
                for hh in range(2):
                    me, other = 64 * hh, 64 - 64 * hh
                    dve.wait_ge(s_qhi, 2 * a + hh + 1)
                    nc.vector.tensor_tensor(q_st[other:other + 64, 2 * a + hh, :], f[me:me + 64],
                                            q_st[me:me + 64, 2 * a + hh, :].bitcast(F32), ALU.subtract
                                            ).then_inc(s_qk, 1)

            def split_k(a):
                f = qk_f[:, a % 2, :]
                for hh in range(2):
                    me = 64 * hh
                    nc.vector.tensor_copy(k_hi[me:me + 64, 2 * a + hh, :], f[me:me + 64]).then_inc(s_qk, 1)
                for hh in range(2):
                    me = 64 * hh
                    dve.wait_ge(s_qk, 4 * a + hh + 1)
                    nc.vector.tensor_tensor(k_lo[me:me + 64, 2 * a + hh, :], f[me:me + 64],
                                            k_hi[me:me + 64, 2 * a + hh, :].bitcast(F32), ALU.subtract
                                            ).then_inc(s_qk, 1)
                    if (a, hh) in KCOPY_DVE:
                        other = 64 - 64 * hh
                        dve.wait_ge(s_qk, 4 * a + hh + 3)
                        nc.vector.tensor_copy(k_lo[other:other + 64, 2 * a + hh, :],
                                              k_lo[me:me + 64, 2 * a + hh, :].bitcast(F32)).then_inc(s_kcd, 1)

            dve.wait_ge(s_keys, EDGE_KEYS)
            dve.wait_ge(s_fill, 9)
            hot_group(0, lo[0], range(0, G // 2))
            dve.wait_ge(s_std, 1)
            factors(0, 0, NT)
            hot_group(0, lo[0], range(G // 2, G))
            hot_group(1, lo[1])
            hi = load_bounds(dve, nc, bounds, 1, NW, EC)
            widest = dve.value_load(bounds[0:1, 2, 0:1], min_val=1, max_val=EC)
            masks()
            for w in range(NW):
                further_groups(w)
                if 1 < w < NW - 2:
                    hot_group(w + 2, lo[w + 2])
                if w == 2:
                    biases()
                if w == 10:
                    dve.wait_ge(s_bhi, 1)
                    nc.vector.tensor_tensor(bhl[BG:BG + R + T, :], b_raw[BG:BG + R + T, :],
                                            bhl[BG:BG + R + T, :].bitcast(F32), ALU.subtract).then_inc(s_blo, 1)
                residual(w)
                for u in side[w]:
                    unit_part(u)
                if w <= 1:
                    hot_group(w + 2, lo[w + 2])

            for u in schedule:
                if u[0] == "sum":
                    it = u[1]
                    dve.wait_ge(s_acc, it + 1)
                    chain(nc.vector.tensor_tensor(self_sum[:, it, :], banks[:, it, :], self_sum[:, it, :],
                                                  ALU.add))
                    chain(nc.vector.scalar_tensor_tensor(out=xs[:, it, :], in0=self_sum[:, it, :], scalar=0.0,
                                                         in1=xs[:, it, :], op0=ALU.max, op1=ALU.add))
                    statistics(1, it).then_inc(s_var, 1)
                elif u[0] == "ln":
                    it = u[1]
                    dve.wait_ge(s_std, 2 + it)
                    factors(1, it, it + 1)
                elif u[0] != "gemm":
                    unit_part(u)

            for step in attention:
                kind, n = step
                if kind == "smax":
                    it, h = divmod(n, H)
                    dve.wait_ge(s_sc, n + 1)
                    dve.wait_ge(s_mask, 2 * (it + 1))
                    if n >= NS:
                        dve.wait_ge(s_exp, n - NS + 1)
                    c = 2 * (n % 2)
                    nc.vector.tensor_tensor_reduce(
                        s_sb[:, n % NS, :].rearrange("p (a j) -> p a j", a=2), banks[:, c:c + 2, 0:HALF],
                        mask_add[:, it, :].rearrange("p (a j) -> p a j", a=2), 1.0, 3.0e38, ALU.add, ALU.min,
                        neg_max[:, it, h:h + 1]).then_inc(s_smax, 1)
                    if n == 1:
                        split_q(KD - 1)
                elif kind == "fill" and n % 2 == 1:
                    dve.wait_ge(s_tr, n + 1)
                    if 4 * n + 3 >= NT * H:
                        dve.wait_ge(s_pv, (4 * n + 3 - NT * H) // (2 * NT) + 1)
                    nc.vector.tensor_copy(pT[:, 4 * n % (NT * H):4 * n % (NT * H) + 4, :],
                                          banks[:, 5 + n % 2, :].rearrange("p (s i) -> p s i", s=4)
                                          ).then_inc(s_ptd, 1)
                elif kind == "norm":
                    dve.wait_ge(s_exp, H * (n + 1))
                    if n >= 2:
                        dve.wait_ge(s_rb, n - 1)
                    chain(nc.vector.reciprocal(recip[:, n % 2, :], denom[:, n, :]))
                    nc.vector.scalar_tensor_tensor(out=norm[:, n % 2, :], in0=neg_max[:, n, :], scalar=BIG / 2,
                                                   in1=recip[:, n % 2, :], op0=ALU.is_lt, op1=ALU.mult
                                                   ).then_inc(s_norm, 1)
                elif kind == "msg":
                    it, a = divmod(n, KD)
                    if a == 0:
                        dve.wait_ge(s_pv, KD * (it + 1))
                        dve.wait_ge(s_rsb, it + 1)
                    if it >= 1:
                        dve.wait_ge(s_mlo, n + 1 - KD)
                    nc.vector.tensor_tensor(msg_f[:, a], banks[:, 4, a * P:(a + 1) * P], r_sb[:, a],
                                            ALU.mult).then_inc(s_msg, 1)
                elif kind == "out":
                    dve.wait_ge(s_ff, n + 1)
                    dve.wait_ge(s_xb, n + 1)
                    if n >= 2:
                        dve.wait_ge(s_out[n % 2], 16 * (n // 2))
                    nc.vector.tensor_tensor(ybuf[:, n % 2, :], banks[:, 7, :], xs[:, n, :], ALU.add
                                            ).then_inc(s_fin, 1)

        @block.tensor
        def _(pe):
            mm = nc.tensor.matmul
            PASSES = ((0, 0), (0, 1), (1, 0))

            pe.wait_ge(s_fill, 4)
            pe.wait_ge(s_keys, 2)
            for k in range(2):
                ins = mm(banks[0:NW, 2, k * EC:(k + 1) * EC], chunk_mm[:, k:k + 1].broadcast_to([EC, NW]),
                         ident[0:EC, 0:EC], start=(k == 0), stop=True, skip_group_check=True)
            ins.then_inc(s_prep, 1)
            pe.wait_ge(s_keys, WINDOW_CHUNKS)
            for k, col in enumerate((2, 1)):
                ins = mm(banks[0:1, 3, k * NW:(k + 1) * NW], win_c[:, col:col + 1], ident[0:NW, 0:NW],
                         start=(k == 0), stop=True, skip_group_check=True)
            ins.then_inc(s_prep, 1)
            for k in range(2):
                nc.tensor.transpose(banks[0:EL, 4, k * EC:(k + 1) * EC], edges_f[:, k, :], ident[0:EC, 0:EC])
            nc.tensor.transpose(banks[:, 4, 160:160 + NT], ntype_f[:], ident[0:NT, 0:NT]).then_inc(s_prep, 1)

            pe.wait_ge(s_keys, BOUNDS)
            pe.wait_ge(s_fill, 16)
            lo = load_bounds(pe, nc, bounds, 0, NW, EC)
            hi = load_bounds(pe, nc, bounds, 1, NW, EC)
            widest = pe.value_load(bounds[0:1, 2, 0:1], min_val=1, max_val=EC)
            filled = [pe.alloc_register(name=f"filled_pe_{i}") for i in range(2)]
            for par in range(2):
                pe.sem_inc(s_slot[par], G)
                pe.reg_mov(filled[par], G // 2)

            def turn(w, first):
                par = w % 2
                for k in range(G):
                    if k % (G // 2) == 0:
                        count = pe.snap(filled[par], min_val=1, max_val=1 << 20)
                        pe.wait_ge(s_src[par], count)
                        pe.wait_ge(s_dst[par], count)
                        pe.reg_add(filled[par], filled[par], G // 2)
                    for jt in range(NT):
                        ins = mm(banks[:, w % 2, jt * R * WIN:(jt + 1) * R * WIN],
                                 src_hot[:, par, k, jt * P:(jt + 1) * P], dst_hot[:, par, k, :],
                                 start=(first and k == 0 and jt == 0), stop=True, skip_group_check=True)
                    ins.then_inc(s_slot[par], 1)

            def window(w):
                if w >= 2:
                    pe.wait_ge(s_res, w - 1)
                turn(w, True)
                with pe.If(hi[w] > lo[w] + G):
                    with pe.Fori(lo[w] + G, hi[w], G):
                        turn(w, False)
                mm(banks[:, w % 2, 500:501], ident16[:], ident16[:, 0:1], start=False, stop=True,
                   skip_group_check=True).then_inc(s_win, 1)

            def adjacency_of(half):
                pe.wait_ge(s_adj, NW // 2 * (half + 1))
                pe.wait_ge(s_res, NW // 2 * (half + 1))

            def take_bank(u):
                if number[u] >= 3:
                    pe.wait_ge(s_ufree, number[u] - 2)

            def unit(u):
                kind = u[0]
                take_bank(u)
                b = bank(u)
                if kind in ("hT", "h2T"):
                    it = u[1]
                    if kind == "hT":
                        pe.wait_ge(s_y0, it + 1)
                        rows = in0[:, it, :]
                    else:
                        pe.wait_ge(s_y, it + 1)
                        rows = ybuf[:, it % 2, :]
                    for kt in range(KD):
                        ins = nc.tensor.transpose(b[:, kt * P:(kt + 1) * P], rows[:, kt * P:(kt + 1) * P], ident[:])
                elif kind == "self":
                    _, t, it = u
                    if it == 0:
                        pe.wait_ge(s_wlo, KD * (t + 1))
                    if t == 0:
                        pe.wait_ge(s_ufree, number[("hT", it, 0)] + 1)
                    ins = gemm(b, hT, it, w_hl[t % 2], 0, D)
                elif kind == "cnt":
                    half = u[1]
                    cols = slice(half * HALF, (half + 1) * HALF)
                    adjacency_of(half)
                    if half == 0:
                        pe.wait_ge(s_keys, MASKS)
                        pe.wait_ge(s_fill, 16)
                    for it in range(NT):
                        a, z = max(it * P, half * HALF), min((it + 1) * P, (half + 1) * HALF)
                        if a < z:
                            mm(b[0:BROWS, a - half * HALF:z - half * HALF], mask6[:, it, :],
                               ident16[:, a - it * P:z - it * P], start=(a == half * HALF), stop=False,
                               skip_group_check=True)
                    with pe.If(widest > EXACT16 // EL):
                        for r in range(R):
                            for jt in range(NT):
                                mm(b[0:BROWS, 0:HALF], sel6[:, r, :], adjT_res[:, jt, r, cols], start=False,
                                   stop=False, skip_group_check=True)
                    for r in range(R):
                        for jt in range(NT):
                            ins = mm(b[0:BROWS, 0:HALF], sel6[:, r, :], adjT[:, jt, r, cols], start=False,
                                     stop=(r == R - 1 and jt == NT - 1), skip_group_check=True)
                elif kind == "z":
                    _, r, dt, half = u
                    cols = slice(half * HALF, (half + 1) * HALF)
                    adjacency_of(half)
                    if (r, dt, half) == (0, 0, 0):
                        pe.wait_ge(s_h16lo, NT)
                    feats = slice(dt * P, (dt + 1) * P)
                    pairs = [(p, jt) for jt in range(NT) for p in range(2)]

                    def add(adj, pick, start, stop):
                        for n, (p, jt) in enumerate(pick):
                            ins = mm(b[:, 0:HALF], h16[:, p, jt, feats], adj[:, jt, r, cols],
                                     start=(start and n == 0), stop=(stop and n == len(pick) - 1),
                                     skip_group_check=True)
                        return ins
                    add(adjT, pairs[:-1], True, False)
                    with pe.If(widest > EXACT16 // EL):
                        add(adjT_res, pairs, False, False)
                    ins = add(adjT, pairs[-1:], False, True)
                elif kind == "m":
                    _, it, part = u
                    tiles = range(4) if part == 0 else range(4, NT)
                    items = [(r, jt) for jt in tiles for r in range(R)]

                    def add(adj, pick, start, stop):
                        for n, (r, jt) in enumerate(pick):
                            rows = (jt - tiles[0]) * P
                            ins = mm(b[:, rows:rows + P], adj[:, jt, r, it * P:(it + 1) * P], ident16[:],
                                     start=(start and n == 0), stop=(stop and n == len(pick) - 1),
                                     skip_group_check=True)
                        return ins
                    add(adjT, items[:-1], True, False)
                    with pe.If(widest > EXACT16 // EL):
                        add(adjT_res, items, False, False)
                    ins = add(adjT, items[-1:], False, True)
                elif kind == "wt":
                    _, g, kt = u
                    q = NWT + g
                    pe.wait_ge(s_raw[q % 2], 16 * (q // 2 + 1))
                    for o in range(4):
                        ins = nc.tensor.transpose(b[:, o * P:(o + 1) * P], raw[q % 2][:, o, kt * P:(kt + 1) * P],
                                                  ident[:])
                elif kind in ("q", "k"):
                    _, a, half = u
                    o = (0 if kind == "q" else D) + a * P
                    if u == ("k", 0, 0):
                        pe.wait_ge(s_ufree, number[("h2T", NT - 1, 0)] + 1)
                    n = 0
                    for kt in range(KD):
                        for pw, ph in PASSES:
                            ins = mm(b[:, 0:HALF], wqkvT[:, pw, kt, o:o + P],
                                     h2T[:, ph, kt, half * HALF:(half + 1) * HALF],
                                     start=(n == 0), stop=(n == 3 * KD - 1))
                            n += 1
                else:
                    pe.wait_ge(s_ufree, number[("h2T", u[1], 0)] + 1)
                    ins = gemm(b, h2T, u[1], wqkvT, 2 * D, D)
                ins.then_inc(s_unit, 1)

            def gemm(to, lhs, it, weights, c0, cn, start=True):
                n = 0
                for kt in range(KD):
                    for pl, pw in PASSES:
                        ins = mm(to, lhs[:, pl, kt, it * P:(it + 1) * P], weights[:, pw, kt, c0:c0 + cn],
                                 start=(start and n == 0), stop=(n == 3 * KD - 1), skip_group_check=True)
                        n += 1
                return ins

            for w in range(NW):
                window(w)
                for u in side[w]:
                    unit(u)
                if w == 1:
                    pe.wait_ge(s_bias, BIASES_IN)
                    nc.tensor.transpose(banks[:, 2, 176:176 + 3 * KD], bqkv_r[:], ident[0:3 * KD, 0:3 * KD]
                                        ).then_inc(s_prep, 1)

            for u in schedule:
                if u[0] in ("sum", "ln"):
                    continue
                if u[0] != "gemm":
                    unit(u)
                    continue
                _, r, it = u
                if it == 0:
                    pe.wait_ge(s_wlo, KD * (T + r + 1))
                    pe.wait_ge(s_ufree, number[("z", r, KD - 1, 1)] + 1)
                if r == 0:
                    if it == 0:
                        pe.wait_ge(s_blo, 1)
                    mm(banks[:, it, :], cnt6[:, it * P:(it + 1) * P], bhl[:], start=True, stop=False,
                       skip_group_check=True)
                ins = gemm(banks[:, it, :], zT[r % 2], it, w_hl[(T + r) % 2], 0, D, start=False)
                if r == R - 1:
                    ins.then_inc(s_acc, 1)
                elif it == NT - 1:
                    ins.then_inc(s_gemm, 1)

            for step in attention:
                kind, n = step
                if kind == "score":
                    it, h = divmod(n, H)
                    if n < H and n % 2 == 0:
                        pe.wait_ge(s_qk, split_count(KD + n // 2 + 1))
                        pe.wait_ge(s_qhi, 2 * (n // 2 + 1))
                    if n == 0:
                        pe.wait_ge(s_kcp, 2 * KD)
                        pe.wait_ge(s_kcl, len(KCOPY_POOL))
                        pe.wait_ge(s_kcd, len(KCOPY_DVE))
                    if n >= 2:
                        pe.wait_ge(s_smax, n - 1)
                    for half in range(2):
                        cols = slice(half * HALF, (half + 1) * HALF)
                        for p, k in enumerate((k_hi, k_lo)):
                            ins = mm(banks[:, 2 * (n % 2) + half, 0:HALF], q_st[:, h, it * P:(it + 1) * P],
                                     k[:, h, cols], start=(p == 0), stop=(p == 1))
                    ins.then_inc(s_sc, 1)
                elif kind == "turn":
                    pe.wait_ge(s_exp, (4 * n + 3) // NT + 1)
                    if n == 0:
                        pe.wait_ge(s_ufree, len(ring))
                    if n >= 2:
                        pe.wait_ge(s_pta if n % 2 == 0 else s_ptd, n // 2)
                    for i in range(4):
                        h, jt = divmod(4 * n + i, NT)
                        ins = nc.tensor.transpose(banks[:, 5 + n % 2, i * P:(i + 1) * P],
                                                  p_sb[:, h % NPR, jt * P:(jt + 1) * P], ident[:])
                    ins.then_inc(s_tr, 1)
                elif kind == "pv":
                    it, a = divmod(n, KD)
                    f = ((2 * n + 2) * NT - 1) // 4
                    pe.wait_ge(s_pta, (f + 2) // 2)
                    pe.wait_ge(s_ptd, (f + 1) // 2)
                    if a == 0 and it >= 1:
                        pe.wait_ge(s_msg, KD * it)
                    for jt in range(NT):
                        for hh in range(2):
                            s = ((2 * n + hh) * NT + jt) % (NT * H)
                            h = 2 * a + hh
                            ins = mm(banks[64 * hh:64 * hh + 64, 4, a * P:(a + 1) * P],
                                     v_sb[:, jt, h * DK:(h + 1) * DK], pT[:, s, :],
                                     start=(jt == 0), stop=(jt == NT - 1), skip_group_check=True)
                    ins.then_inc(s_pv, 1)
                elif kind == "rb":
                    pe.wait_ge(s_norm, n + 1)
                    if n >= 1:
                        pe.wait_ge(s_fin, n)
                    for h in range(H):
                        me = 64 * (h % 2)
                        ins = mm(banks[me:me + 64, 7, h // 2 * P:(h // 2 + 1) * P],
                                 norm[:, n % 2, h:h + 1].broadcast_to([P, DK]), ident[:],
                                 start=(h < 2), stop=True, skip_group_check=True)
                    ins.then_inc(s_rb, 1)
                elif kind == "ff":
                    it, kt = divmod(n, KD)
                    pe.wait_ge(s_mlo, n + 1)
                    if kt == 0:
                        pe.wait_ge(s_rsb, it + 1)
                    for k, (pl, pw) in enumerate(PASSES):
                        ins = mm(banks[:, 7, :], msgT[:, it % 2, pl, kt, :], wffT[:, pw, kt, :],
                                 start=(kt == 0 and k == 0), stop=(kt == KD - 1 and k == len(PASSES) - 1),
                                 skip_group_check=True)
                    if kt == KD - 1:
                        ins.then_inc(s_ff, 1)


def load_bounds(eng, nc, bounds, row, nw, last):
    _, values = nc.values_load_multi_w_load_instructions(
        bounds[0:1, row, 0:nw], engines=(eng.engine,), min_val=0, max_val=last,
        skip_runtime_bounds_check_because="the vector engine clamped them")
    return values


INPUTS = ["x", "src", "dst", "edge_type_3", "node_type_3", "L0_gnn_W_rel", "L0_gnn_b_rel", "L0_gnn_W_self",
          "L0_gnn_b_self", "L1_gnn_W_qkv", "L1_gnn_b_qkv", "L1_gnn_W_ff", "L1_gnn_b_ff"]


def kernel(**inputs):
    import numpy as np
    import concourse.bacc as bacc
    from concourse.bass_utils import run_bass_kernel_spmd

    nc = bacc.Bacc("TRN2", target_bir_lowering=False, num_devices=1)
    arrays, args = {}, []
    for name in INPUTS:
        a = np.ascontiguousarray(inputs[name])
        arrays[f"in_{name}_dram"] = a
        args.append(nc.dram_tensor(f"in_{name}_dram", a.shape, mybir.dt.from_np(a.dtype), kind="ExternalInput").ap())
    shape = inputs["x"].shape
    args.append(nc.dram_tensor("out_0_dram", shape, F32, kind="ExternalOutput").ap())
    gnn_kernel(nc, *args)
    result = run_bass_kernel_spmd(nc, [arrays], core_ids=[0])
    return result.results[0]["out_0_dram"]
```
